# Optimizing a Trainium2 kernel written in Bass

```python
import numpy as np
import jax
import jax.numpy as jnp

def _softmax(x, axis=-1):
    return jax.nn.softmax(x, axis=axis)

def _gelu(x):
    return jax.nn.gelu(x, approximate=True)

def _silu(x):
    return jax.nn.silu(x)

def _sigmoid(x):
    return jax.nn.sigmoid(x)

def _layernorm(x, axis=-1, eps=1e-05):
    m = jnp.mean(x, axis=axis, keepdims=True)
    v = jnp.var(x, axis=axis, keepdims=True)
    return (x - m) / jnp.sqrt(v + eps)

def _scatter_add(tgt, idx, src, axis=0):
    return tgt.at[idx].add(src)

def _segment_sum(src, seg, n):
    return jax.ops.segment_sum(src, seg, n)
kernel_name = 'mk_seq_postln_d1_jaxref_r8_4a5c0c'

def setup_inputs(seed: int=0):
    np.random.seed(seed)
    _w = jnp.asarray

    def _L0_attn_setup():
        import jax, jax.numpy as jnp
        import numpy as np
        B, T, C, NF = (8, 256, 128, 64)
        EPS = 1e-06

        def mmnorm(x):
            return x / (jnp.max(jnp.abs(x), axis=-1, keepdims=True) + EPS)

        def _scanner(y, x, freq_W, freq_b, out_W, out_b):
            z = jnp.concatenate([y, x], axis=-1)
            f = z @ freq_W + freq_b
            z = jnp.concatenate([jnp.sin(f), jnp.cos(f)], -1) @ out_W + out_b
            return mmnorm(z)
        key = jax.random.key(seed)
        ks = jax.random.split(key, 8)

        def w(k, shape, fan_in):
            return jax.random.normal(k, shape, jnp.float32) * (1.0 / np.sqrt(fan_in))
        return {'x': jax.random.normal(ks[0], (B, T, C), jnp.float32), 'attn_W': w(ks[1], (C, 2 * C), C), 'attn_b': jnp.zeros((2 * C,), jnp.float32), 'freq_W': w(ks[2], (2 * C, NF), 2 * C), 'freq_b': jnp.zeros((NF,), jnp.float32), 'out_W': w(ks[3], (2 * NF, C), 2 * NF), 'out_b': jnp.zeros((C,), jnp.float32), 'proj_W': w(ks[4], (C, C), C), 'proj_b': jnp.zeros((C,), jnp.float32), 'identity': jax.random.uniform(ks[5], (C,), jnp.float32)}
    _L0_attn_in = _L0_attn_setup()

    def _L0_ffn_setup():
        import jax, jax.numpy as jnp
        import numpy as np
        TOP_K = 2
        key = jax.random.key(seed)
        k1, k2, k3, k4 = jax.random.split(key, 4)
        B, S, H, I, E = (2, 256, 128, 512, 8)
        return {'hidden_states': jax.random.normal(k1, (B, S, H), jnp.float32), 'gate_w': jax.random.normal(k2, (E, H), jnp.float32) * 0.02, 'gate_up_proj': jax.random.normal(k3, (E, 2 * I, H), jnp.float32) * 0.02, 'down_proj': jax.random.normal(k4, (E, H, I), jnp.float32) * 0.02}
    _L0_ffn_in = _L0_ffn_setup()
    _d = {'L0_attn_x': _L0_attn_in['x'], 'L0_attn_attn_W': _L0_attn_in['attn_W'], 'L0_attn_attn_b': _L0_attn_in['attn_b'], 'L0_attn_freq_W': _L0_attn_in['freq_W'], 'L0_attn_freq_b': _L0_attn_in['freq_b'], 'L0_attn_out_W': _L0_attn_in['out_W'], 'L0_attn_out_b': _L0_attn_in['out_b'], 'L0_attn_proj_W': _L0_attn_in['proj_W'], 'L0_attn_proj_b': _L0_attn_in['proj_b'], 'L0_attn_identity': _L0_attn_in['identity'], 'L0_ffn_gate_w': _L0_ffn_in['gate_w'], 'L0_ffn_gate_up_proj': _L0_ffn_in['gate_up_proj'], 'L0_ffn_down_proj': _L0_ffn_in['down_proj']}
    _x0 = _d['L0_attn_x']
    _d['L0_attn_x'] = jax.random.normal(jax.random.fold_in(jax.random.key(seed), 1), (8, 512, 128), dtype=_x0.dtype)
    del _x0
    return _d

def reference(L0_attn_x, L0_attn_attn_W, L0_attn_attn_b, L0_attn_freq_W, L0_attn_freq_b, L0_attn_out_W, L0_attn_out_b, L0_attn_proj_W, L0_attn_proj_b, L0_attn_identity, L0_ffn_gate_w, L0_ffn_gate_up_proj, L0_ffn_down_proj):

    def _L0_attn_ref(x, attn_W, attn_b, freq_W, freq_b, out_W, out_b, proj_W, proj_b, identity):
        import jax, jax.numpy as jnp
        import numpy as np
        B, T, C, NF = (8, 256, 128, 64)
        EPS = 1e-06

        def mmnorm(x):
            return x / (jnp.max(jnp.abs(x), axis=-1, keepdims=True) + EPS)

        def _scanner(y, x, freq_W, freq_b, out_W, out_b):
            z = jnp.concatenate([y, x], axis=-1)
            f = z @ freq_W + freq_b
            z = jnp.concatenate([jnp.sin(f), jnp.cos(f)], -1) @ out_W + out_b
            return mmnorm(z)
        b, t, c = x.shape
        qv = x @ attn_W + attn_b
        q, v = (qv[..., :c], qv[..., c:])
        n = 1
        while n < t:
            prev = jnp.concatenate([jnp.broadcast_to(identity, (b, n, c)), q[:, :t - n]], axis=1)
            q = _scanner(prev, q, freq_W, freq_b, out_W, out_b)
            n *= 2
        Y = q * v
        return Y @ proj_W + proj_b

    def _L0_ffn_ref(hidden_states, gate_w, gate_up_proj, down_proj):
        import jax, jax.numpy as jnp
        import numpy as np
        TOP_K = 2
        B, S, H = hidden_states.shape
        E = gate_w.shape[0]
        x = hidden_states.reshape(-1, H)
        T = x.shape[0]
        probs = jax.nn.softmax(x @ gate_w.T, axis=-1)
        w, idx = jax.lax.top_k(probs, TOP_K)
        w = w / jnp.sum(w, axis=-1, keepdims=True)
        combine = jnp.zeros((T, E), x.dtype).at[jnp.arange(T)[:, None], idx].add(w)

        def step(acc, inputs):
            gup, dn, ce = inputs
            g, u = jnp.split(x @ gup.T, 2, axis=-1)
            acc = acc + ce[:, None] * (jax.nn.silu(g) * u @ dn.T)
            return (acc, None)
        out, _ = jax.lax.scan(step, jnp.zeros_like(x), (gate_up_proj, down_proj, combine.T))
        return out.reshape(B, S, H)
    x = L0_attn_x
    x = _layernorm(x + _L0_attn_ref(x, L0_attn_attn_W, L0_attn_attn_b, L0_attn_freq_W, L0_attn_freq_b, L0_attn_out_W, L0_attn_out_b, L0_attn_proj_W, L0_attn_proj_b, L0_attn_identity), axis=-1)
    x = _layernorm(x + _L0_ffn_ref(x, L0_ffn_gate_w, L0_ffn_gate_up_proj, L0_ffn_down_proj), axis=-1)
    return x

_drawn_inputs = setup_inputs


def setup_inputs(seed=0):
    import zlib

    import numpy as np

    out = dict(_drawn_inputs(seed))
    spreads = {'L0_attn_attn_b': (0.0, 0.1),
     'L0_attn_freq_b': (0.0, 0.1),
     'L0_attn_out_b': (0.0, 0.1),
     'L0_attn_proj_b': (0.0, 0.1)}
    factors = {'L0_ffn_gate_w': 7.786, 'L0_ffn_gate_up_proj': 6.804, 'L0_ffn_down_proj': 6.815}
    for name, (base, spread) in spreads.items():
        noise = np.random.default_rng([zlib.crc32(name.encode()), seed]).standard_normal(out[name].shape)
        drawn = base * np.exp(spread * noise) if base else spread * noise
        out[name] = jnp.asarray(drawn.astype(out[name].dtype))
    for name, factor in factors.items():
        out[name] = (out[name] * factor).astype(out[name].dtype)
    return out
```

```python
from contextlib import ExitStack

import concourse.bass as bass
from concourse import mybir

ALU = mybir.AluOpType
ACT = mybir.ActivationFunctionType
AX = mybir.AxisListType
F32 = mybir.dt.float32
BF16 = mybir.dt.bfloat16
I32 = mybir.dt.int32
U32 = mybir.dt.uint32

P = 128
NSEQ, LEN, C = 8, 512, 128
STEPS = 9
PAD = LEN // 2
CH = LEN // P
NT = NSEQ * CH
E, HID = 8, 512
HC = HID // P
TOPK = 2
TILES = NT * TOPK + E
ITEMS = STEPS * NSEQ
PEEL = 4
EPS_MAX, EPS_LN = 1e-6, 1e-5
MAGIC = 1.5 * 2.0 ** 23
INV_TWO_PI = 0.15915494309189535
TWO_PI = 6.2831850
NEG = -3.0e38


def build(nc, x_rows, x_cols, attn_W, attn_bq, attn_bv, freq_W, freq_b, out_W, out_b, proj_W, proj_b,
          ident_col, gate_T, gu_T, dn_T, out):
    ctx = ExitStack()
    with ctx:
        def sb(name, shape, dt=F32):
            return ctx.enter_context(nc.sbuf_tensor(name, shape, dt))

        def ps(name, shape, dt=F32):
            return ctx.enter_context(nc.psum_tensor(name, shape, dt))

        def sem(name):
            return ctx.enter_context(nc.semaphore(name))

        w_attn = sb("w_attn", [P, 2 * C])
        b_q = sb("b_q", [P, 1])
        b_v = sb("b_v", [P, 1])
        w_freq_raw = sb("w_freq_raw", [P, 2, P])
        w_freq = sb("w_freq", [P, 2, P])
        w_out = sb("w_out", [P, C])
        w_proj = sb("w_proj", [P, C])
        w_gate = sb("w_gate", [P, E])
        w_gu = sb("w_gu", [P, E, 2 * HID])
        w_dn = sb("w_dn", [P, E, HC, C])
        bias_row = sb("bias_row", [1, 3, P])
        bias_f = sb("bias_f", [1, P])
        left = sb("left", [1, 2, P])
        bias_split = sb("bias_split", [P, 3, P], BF16)
        ones_bf = sb("ones_bf", [P, LEN], BF16)
        iota_p = sb("iota_p", [P, P])
        identity = sb("identity", [P, P])
        before = sb("before", [P, P], BF16)
        idc = sb("idc", [P, 1])
        xT = sb("xT", [P, NT, P])
        x1 = sb("x1", [P, NT, C])
        q = sb("q", [P, NSEQ, PAD + LEN])
        vT = sb("vT", [P, NSEQ, LEN])
        turns_rounded = sb("turns_rounded", [P, 2, LEN])
        turns = sb("turns", [P, 2, LEN])
        waves = sb("waves", [P, 2, LEN])
        z_scaled = sb("z_scaled", [P, 2, CH, C])
        z_max = sb("z_max", [P, 2, CH])
        z_max_eps = sb("z_max_eps", [P, 2, CH])
        z_inv = sb("z_inv", [P, 2, CH])
        gated = sb("gated", [P, 2, LEN])
        stats = sb("stats", [P, NT, 6])
        mean_var = sb("mean_var", [P, NT, 2])
        std = sb("std", [P, NT])
        rstd = sb("rstd", [P, NT])
        logits = sb("logits", [P, NT, E])
        shifted = sb("shifted", [P, NT, E])
        probs = sb("probs", [P, NT, E])
        rank_key = sb("rank_key", [P, NT, E])
        work = sb("work", [P, NT, E])
        pick = [sb(f"pick{k}", [P, NT, E]) for k in range(TOPK)]
        masked = sb("masked", [P, NT, E])
        picked = sb("picked", [P, NT, E], BF16)
        col = sb("col", [P, NT])
        weight_raw = sb("weight_raw", [P, TOPK, NT])
        weight = sb("weight", [P, TOPK, NT])
        wsum = sb("wsum", [P, NT])
        tile_count = sb("tile_count", [P, NT, E])
        ones_f = sb("ones_f", [P, NT])
        count_to = sb("count_to", [P, NT, E])
        place = sb("place", [P, NT, E])
        e_tiles = sb("e_tiles", [P, E])
        e_tiles_r = sb("e_tiles_r", [P, E])
        e_end = sb("e_end", [P, E])
        e_base = sb("e_base", [P, E])
        pos_f = sb("pos_f", [P, TOPK, NT])
        pos = sb("pos", [P, TOPK, NT], U32)
        tile_no = sb("tile_no", [1, TILES, E])
        tile_ge = sb("tile_ge", [1, TILES, E])
        tile_expert_f = sb("tile_expert_f", [1, TILES])
        tile_expert = sb("tile_expert", [1, TILES], I32)
        zeros = sb("zeros", [P, 8, C])
        row_tile = sb("row_tile", [P, 2, C])
        col_tile = sb("col_tile", [P, 2, P])
        act_gate = sb("act_gate", [P, 2, HID])
        hidden = sb("hidden", [P, 2, HID])
        hidden_T = sb("hidden_T", [P, HC, P])
        y_tile = sb("y_tile", [P, 2, C])
        y_back = sb("y_back", [P, 4, TOPK, C])
        part = sb("part", [P, 2, C])
        res = sb("res", [P, 4, C])
        stats2 = sb("stats2", [P, 2, 6])
        mean_var2 = sb("mean_var2", [P, 4, 2])
        std2 = sb("std2", [P, 4])
        rstd2 = sb("rstd2", [P, 4])
        out_tile = sb("out_tile", [P, 4, C])
        eps_ln = sb("eps_ln", [P, 1])

        bank = [ps(f"bank{i}", [P, LEN]) for i in range(8)]
        F, Z, T = bank[0:2], bank[2:4], bank[4:6]

        sorted_x = nc.dram_tensor("sorted_x", [TILES * P, C], F32, kind="Internal").ap()
        sorted_y = nc.dram_tensor("sorted_y", [TILES * P, C], F32, kind="Internal").ap()

        loaded_small = sem("loaded_small")
        loaded_xT = sem("loaded_xT")
        loaded_rows = sem("loaded_rows")
        loaded_experts = sem("loaded_experts")
        iota_done = sem("iota_done")
        const_step = sem("const_step")
        consts_ready = sem("consts_ready")
        zeros_ready = sem("zeros_ready")
        zeros_sent = sem("zeros_sent")
        q0_done = sem("q0_done")
        v0_done = sem("v0_done")
        v_ready = sem("v_ready")
        q_ready = sem("q_ready")
        f_done = sem("f_done")
        rounded = sem("rounded")
        turns_ready = sem("turns_ready")
        waves_ready = sem("waves_ready")
        z_done = sem("z_done")
        scale_step = sem("scale_step")
        scaled = sem("scaled")
        turned = sem("turned")
        gated_ready = sem("gated_ready")
        proj_done = sem("proj_done")
        res_ready = sem("res_ready")
        norm_step = sem("norm_step")
        std_ready = sem("std_ready")
        x1_ready = sem("x1_ready")
        x1T_done = sem("x1T_done")
        x1T_ready = sem("x1T_ready")
        logits_done = sem("logits_done")
        route_step = sem("route_step")
        exp_done = sem("exp_done")
        counts_done = sem("counts_done")
        picked_ready = sem("picked_ready")
        shifted_ready = sem("shifted_ready")
        routed = sem("routed")
        sent = sem("sent")
        row_loaded = [sem(f"row_loaded{k}") for k in range(2)]
        row_turned = sem("row_turned")
        col_ready = sem("col_ready")
        gate_done = sem("gate_done")
        up_done = sem("up_done")
        act_ready = sem("act_ready")
        hidden_ready = sem("hidden_ready")
        hidden_turned = sem("hidden_turned")
        hidden_T_ready = sem("hidden_T_ready")
        y_done = sem("y_done")
        y_ready = sem("y_ready")
        y_stored = [sem(f"y_stored{k}") for k in range(2)]
        y_fetched = [sem(f"y_fetched{k}") for k in range(4)]
        merge_step = sem("merge_step")
        var_ready = sem("var_ready")
        std2_ready = sem("std2_ready")
        out_ready = sem("out_ready")
        out_stored = [sem(f"out_stored{k}") for k in range(4)]

        block = ctx.enter_context(nc.Block())
        SMALL = 12

        @block.sync
        def _(sp):
            for dst, src in ((w_attn[:, :], attn_W), (b_q[:, :], attn_bq), (b_v[:, :], attn_bv),
                             (w_freq_raw[:, :, :], freq_W), (w_out[:, :], out_W), (w_proj[:, :], proj_W),
                             (w_gate[:, :], gate_T), (bias_row[:, 0, :], freq_b), (bias_row[:, 1, :], out_b),
                             (bias_row[:, 2, :], proj_b), (idc[:, :], ident_col)):
                sp.dma_start(dst, src).then_inc(loaded_small, 16)
            for b in range(NSEQ):
                sp.dma_start(xT[:, b * CH:(b + 1) * CH, :], x_cols[:, b * LEN:(b + 1) * LEN].rearrange(
                    "c (t p) -> c t p", p=P)).then_inc(loaded_xT, 16)
            sp.dma_start(x1[:, :, :], x_rows).then_inc(loaded_rows, 16)
            sp.dma_start(w_gu[:, :, :], gu_T).then_inc(loaded_experts, 16)
            sp.dma_start(w_dn[:, :, :, :], dn_T).then_inc(loaded_experts, 16)
            sp.wait_ge(zeros_ready, 1)
            for g in range(TILES // 8):
                sp.dma_start(sorted_x[g * 8 * P:(g + 1) * 8 * P, :].rearrange("(p t) c -> p t c", t=8),
                             zeros[:, :, :]).then_inc(zeros_sent, 16)
            sp.wait_ge(sent, 16 * TOPK * NT)
            for k in range(2):
                sp.dma_start(row_tile[:, k, :], sorted_x[k * P:(k + 1) * P, :]).then_inc(row_loaded[k], 16)
            with sp.Fori(0, TILES // 2 - 1) as g:
                for k in range(2):
                    i = g * 2 + k
                    sp.wait_ge(row_turned, i + 1)
                    sp.dma_start(row_tile[:, k, :], sorted_x[bass.ds((i + 2) * P, P), :]).then_inc(row_loaded[k], 16)
            with sp.Fori(0, NT // 4) as g:
                for k in range(4):
                    j = g * 4 + k
                    sp.wait_ge(out_ready, j + 1)
                    sp.dma_start(out[bass.ds(j * P, P), :], out_tile[:, k, :]).then_inc(out_stored[k], 16)
            for k in range(4):
                sp.wait_ge(out_stored[k], 16 * (NT // 4))
            sp.wait_ge(zeros_sent, 16 * (TILES // 8))

        @block.gpsimd
        def _(pool):
            nc.gpsimd.iota(iota_p[:, :], pattern=[[1, P]], base=0, channel_multiplier=-1,
                           allow_small_or_imprecise_dtypes=True).then_inc(iota_done, 1)
            nc.gpsimd.iota(tile_no[:, :, :], pattern=[[1, TILES], [0, E]], base=0, channel_multiplier=0,
                           allow_small_or_imprecise_dtypes=True).then_inc(iota_done, 1)
            nc.gpsimd.iota(rank_key[:, :, :], pattern=[[0, NT], [-1, E]], base=E, channel_multiplier=0,
                           allow_small_or_imprecise_dtypes=True).then_inc(iota_done, 1)
            nc.gpsimd.memset(zeros[:, :, :], 0.0).then_inc(zeros_ready, 1)
            pool.wait_ge(zeros_sent, 16 * (TILES // 8))
            pool.wait_ge(routed, 1)
            pool.wait_ge(x1_ready, NT)
            for j in range(NT):
                for k in range(TOPK):
                    nc.gpsimd.indirect_dma_start(
                        out=sorted_x, out_offset=bass.IndirectOffsetOnAxis(ap=pos[:, k, j:j + 1], axis=0),
                        in_=x1[:, j, :], in_offset=None).then_inc(sent, 16)
            with pool.Fori(0, TILES // 2) as g:
                for k in range(2):
                    i = g * 2 + k
                    pool.wait_ge(y_ready, i + 1)
                    pool.dma_start(sorted_y[bass.ds(i * P, P), :], y_tile[:, k, :]).then_inc(y_stored[k], 16)
            for k in range(2):
                pool.wait_ge(y_stored[k], 16 * (TILES // 2))
            for j in range(NT):
                if j >= 4:
                    pool.wait_ge(var_ready, j - 3)
                for k in range(TOPK):
                    nc.gpsimd.indirect_dma_start(
                        out=y_back[:, j % 4, k, :], out_offset=None,
                        in_=sorted_y, in_offset=bass.IndirectOffsetOnAxis(ap=pos[:, k, j:j + 1], axis=0),
                    ).then_inc(y_fetched[j % 4], 16)

        @block.tensor
        def _(pe):
            pe.wait_ge(loaded_small, 16 * 11)
            for b in range(NSEQ):
                pe.wait_ge(loaded_xT, 16 * NSEQ)
                if b >= 2:
                    pe.wait_ge(q_ready, b - 1)
                cols = xT[:, b * CH:(b + 1) * CH, :]
                nc.tensor.matmul(F[b % 2][:, :], w_attn[:, 0:C], cols, start=True, stop=True).then_inc(q0_done, 1)
                if b >= 2:
                    pe.wait_ge(v_ready, b - 1)
                nc.tensor.matmul(Z[b % 2][:, :], w_attn[:, C:2 * C], cols, start=True, stop=True).then_inc(v0_done, 1)
            pe.wait_ge(q_ready, NSEQ)
            pe.wait_ge(v_ready, NSEQ)
            pe.wait_ge(consts_ready, 1)

            def angles(m, b, shift):
                k = b % 2
                nc.tensor.matmul(F[k][:, :], bias_split[:, 0, :], ones_bf[:, :], start=True, stop=False)
                nc.tensor.matmul(F[k][:, :], w_freq[:, 0, :], q[:, b, bass.ds(PAD - shift, LEN)], start=False, stop=False)
                nc.tensor.matmul(F[k][:, :], w_freq[:, 1, :], q[:, b, PAD:PAD + LEN],
                                 start=False, stop=True).then_inc(f_done, 1)

            def mix(m, b):
                k = b % 2
                nc.tensor.matmul(Z[k][:, :], ones_bf[:, 0:P], bias_split[:, 1:2, :].broadcast_to([P, CH, P]),
                                 start=True, stop=False, skip_group_check=True)
                for c in range(CH):
                    last = nc.tensor.matmul(Z[k][:, c * P:(c + 1) * P], waves[:, k, c * P:(c + 1) * P], w_out[:, :],
                                            start=False, stop=(c == CH - 1), skip_group_check=True)
                last.then_inc(z_done, 1)

            def turn(b):
                k = b % 2
                for c in range(CH):
                    last = nc.tensor.transpose(T[k][:, c * P:(c + 1) * P], z_scaled[:, k, c, :], identity[:, :])
                last.then_inc(turned, 1)

            for b in range(NSEQ):
                if b >= 2:
                    pe.wait_ge(turns_ready, b - 1)
                angles(b, b, 1)
                if b >= 1:
                    pe.wait_ge(waves_ready, b)
                    if b >= 3:
                        pe.wait_ge(scaled, b - 2)
                    mix(b - 1, b - 1)
                if b >= 2:
                    pe.wait_ge(scaled, b - 1)
                    if b >= 4:
                        pe.wait_ge(q_ready, NSEQ + b - 3)
                    turn(b - 2)
            with pe.Fori(1, STEPS) as s:
                for b in range(NSEQ):
                    m = s * NSEQ + b
                    pe.wait_ge(q_ready, m + 1)
                    pe.wait_ge(turns_ready, m - 1)
                    angles(m, b, 1 << s)
                    pe.wait_ge(waves_ready, m)
                    pe.wait_ge(scaled, m - 2)
                    mix(m - 1, (b - 1) % NSEQ)
                    pe.wait_ge(scaled, m - 1)
                    pe.wait_ge(q_ready, m + NSEQ - 3)
                    turn((b - 2) % NSEQ)
            pe.wait_ge(waves_ready, ITEMS)
            pe.wait_ge(scaled, ITEMS - 2)
            mix(ITEMS - 1, NSEQ - 1)
            for b in (NSEQ - 2, NSEQ - 1):
                m = ITEMS - NSEQ + b
                pe.wait_ge(scaled, m + 1)
                pe.wait_ge(q_ready, m + NSEQ - 1)
                turn(b)

            for b in range(NSEQ):
                k = b % 2
                pe.wait_ge(gated_ready, b + 1)
                if b < 2:
                    pe.wait_ge(turns_ready, ITEMS)
                else:
                    pe.wait_ge(res_ready, b - 1)
                nc.tensor.matmul(F[k][:, :], ones_bf[:, 0:P], bias_split[:, 2:3, :].broadcast_to([P, CH, P]),
                                 start=True, stop=False, skip_group_check=True)
                for c in range(CH):
                    last = nc.tensor.matmul(F[k][:, c * P:(c + 1) * P], gated[:, k, c * P:(c + 1) * P], w_proj[:, :],
                                            start=False, stop=(c == CH - 1), skip_group_check=True)
                last.then_inc(proj_done, 1)

            def gate(b):
                pe.wait_ge(x1T_ready, b + 1)
                for c in range(CH):
                    j = b * CH + c
                    last = nc.tensor.matmul(bank[6][:, j * E:(j + 1) * E], xT[:, j, :], w_gate[:, :],
                                            start=True, stop=True, skip_group_check=True)
                if b == NSEQ - 1:
                    last.then_inc(logits_done, 1)

            pe.wait_ge(q_ready, NSEQ + ITEMS)
            for b in range(NSEQ):
                pe.wait_ge(x1_ready, (b + 1) * CH)
                if b >= 2:
                    pe.wait_ge(x1T_ready, b - 1)
                for c in range(CH):
                    last = nc.tensor.transpose(T[b % 2][:, c * P:(c + 1) * P], x1[:, b * CH + c, :], identity[:, :])
                last.then_inc(x1T_done, 1)
                if b >= 1:
                    gate(b - 1)
            gate(NSEQ - 1)
            pe.wait_ge(picked_ready, 1)
            nc.tensor.matmul(bank[7][:, 0:NT * E], before[:, :], picked[:, :, :], start=True, stop=True)\
                .then_inc(counts_done, 1)
            pe.wait_ge(res_ready, NSEQ)
            nc.tensor.matmul(F[0][:, 0:NT * E], ones_bf[:, 0:P], picked[:, :, :], start=True, stop=True)\
                .then_inc(counts_done, 1)

            pe.wait_ge(routed, 1)
            pe.wait_ge(loaded_experts, 32)

            def turn_rows(k):
                nc.tensor.transpose(bank[6][:, 0:P], row_tile[:, k, :], identity[:, :]).then_inc(row_turned, 1)

            def gate_up(k, e, half):
                nc.tensor.matmul(bank[2 * half + k][:, :], col_tile[:, k, :],
                                 w_gu[:, bass.ds(e, 1), half * HID:(half + 1) * HID].rearrange("p a n -> p (a n)"),
                                 start=True, stop=True).then_inc((gate_done, up_done)[half], 1)

            def turn_hidden(k):
                for c in range(HC):
                    last = nc.tensor.transpose(bank[4][:, c * P:(c + 1) * P], hidden[:, k, c * P:(c + 1) * P],
                                               identity[:, :])
                last.then_inc(hidden_turned, 1)

            def down(e):
                for c in range(HC):
                    last = nc.tensor.matmul(bank[5][:, 0:C], hidden_T[:, c, :],
                                            w_dn[:, bass.ds(e, 1), c, :].rearrange("p a n -> p (a n)"),
                                            start=(c == 0), stop=(c == HC - 1))
                last.then_inc(y_done, 1)

            def expert_of(i):
                return pe.value_load(tile_expert[0:1, bass.ds(i, 1)], min_val=0, max_val=E - 1)

            def slot(i, pair, k):
                if not isinstance(i, int) or i + 1 < TILES:
                    pe.wait_ge(row_loaded[1 - k], (pair + k + 1) * 16)
                    pe.wait_ge(col_ready, i + 1)
                    turn_rows(1 - k)
                pe.wait_ge(col_ready, i + 1)
                e = expert_of(i)
                if not isinstance(i, int) or i >= 2:
                    pe.wait_ge(act_ready, i - 1)
                gate_up(k, e, 0)
                if not isinstance(i, int) or i >= 1:
                    pe.wait_ge(hidden_ready, i)
                    turn_hidden(1 - k)
                gate_up(k, e, 1)
                if not isinstance(i, int) or i >= 1:
                    finish(i - 1)

            def finish(i):
                e = expert_of(i)
                pe.wait_ge(hidden_T_ready, i + 1)
                if not isinstance(i, int) or i >= 1:
                    pe.wait_ge(y_ready, i)
                down(e)

            pe.wait_ge(row_loaded[0], 16)
            turn_rows(0)
            for i in range(PEEL):
                slot(i, i // 2, i % 2)
            with pe.Fori(PEEL // 2, TILES // 2 - 1) as pair:
                for k in range(2):
                    slot(pair * 2 + k, pair, k)
            for i in range(TILES - 2, TILES):
                slot(i, i // 2, i % 2)
            pe.wait_ge(hidden_ready, TILES)
            turn_hidden(1)
            finish(TILES - 1)

        @block.scalar
        def _(act):
            act.wait_ge(loaded_small, 16 * 11)
            for b in range(NSEQ):
                act.wait_ge(q0_done, b + 1)
                nc.scalar.activation(q[:, b, PAD:PAD + LEN], F[b % 2][:, :], ACT.Identity,
                                     bias=b_q[:, 0:1]).then_inc(q_ready, 1)

            def round_turns(k):
                nc.scalar.activation(turns_rounded[:, k, :], F[k][:, :], ACT.Copy, bias=MAGIC).then_inc(rounded, 1)

            def wave(k):
                nc.scalar.activation(waves[:, k, :], turns[:, k, :], ACT.Sin, scale=-TWO_PI).then_inc(waves_ready, 1)

            def take_q(b):
                nc.scalar.activation(q[:, b, PAD:PAD + LEN], T[b % 2][:, :], ACT.Copy).then_inc(q_ready, 1)

            for b in range(NSEQ):
                act.wait_ge(f_done, b + 1)
                if b >= 2:
                    act.wait_ge(turns_ready, b - 1)
                round_turns(b % 2)
                if b >= 2:
                    act.wait_ge(turned, b - 1)
                    take_q(b - 2)
                act.wait_ge(turns_ready, b + 1)
                if b >= 2:
                    act.wait_ge(z_done, b - 1)
                wave(b % 2)
            with act.Fori(1, STEPS) as s:
                for b in range(NSEQ):
                    m = s * NSEQ + b
                    act.wait_ge(f_done, m + 1)
                    act.wait_ge(turns_ready, m - 1)
                    round_turns(b % 2)
                    act.wait_ge(turned, m - 1)
                    take_q((b - 2) % NSEQ)
                    act.wait_ge(turns_ready, m + 1)
                    act.wait_ge(z_done, m - 1)
                    wave(b % 2)
            for b in (NSEQ - 2, NSEQ - 1):
                act.wait_ge(turned, ITEMS - NSEQ + b + 1)
                take_q(b)

            act.wait_ge(norm_step, NT)
            nc.scalar.activation(std[:, :], mean_var[:, :, 1], ACT.Sqrt, bias=eps_ln[:, 0:1]).then_inc(std_ready, 1)
            for b in range(NSEQ):
                act.wait_ge(x1T_done, b + 1)
                nc.scalar.activation(xT[:, b * CH:(b + 1) * CH, :].rearrange("p t c -> p (t c)"), T[b % 2][:, :],
                                     ACT.Copy).then_inc(x1T_ready, 1)
            act.wait_ge(shifted_ready, 1)
            nc.scalar.activation(probs[:, :, :], shifted[:, :, :], ACT.Exp).then_inc(exp_done, 1)

            def silu(k):
                nc.scalar.activation(act_gate[:, k, :], bank[k][:, :], ACT.Silu).then_inc(act_ready, 1)

            def take_y(k):
                nc.scalar.activation(y_tile[:, k, :], bank[5][:, 0:C], ACT.Copy).then_inc(y_ready, 1)

            def slot(i, pair, k):
                act.wait_ge(gate_done, i + 1)
                if not isinstance(i, int) or i >= 2:
                    act.wait_ge(hidden_ready, i - 1)
                silu(k)
                if not isinstance(i, int) or i >= 1:
                    finish(i - 1, pair + k - 1, 1 - k)

            def finish(i, before_it, k):
                act.wait_ge(y_done, i + 1)
                if not isinstance(i, int) or i >= 2:
                    act.wait_ge(y_stored[k], before_it * 16)
                take_y(k)

            for i in range(PEEL):
                slot(i, i // 2, i % 2)
            with act.Fori(PEEL // 2, TILES // 2 - 1) as pair:
                for k in range(2):
                    slot(pair * 2 + k, pair, k)
            for i in range(TILES - 2, TILES):
                slot(i, i // 2, i % 2)
            finish(TILES - 1, TILES // 2 - 1, 1)

            for j in range(NT):
                act.wait_ge(var_ready, j + 1)
                if j >= 4:
                    act.wait_ge(out_ready, j - 3)
                nc.scalar.activation(std2[:, j % 4:j % 4 + 1], mean_var2[:, j % 4, 1:2], ACT.Sqrt,
                                     bias=eps_ln[:, 0:1]).then_inc(std2_ready, 1)

        @block.vector
        def _(dve):
            made = [0]

            def const(ins):
                made[0] += 1
                ins.then_inc(const_step, 1)

            def settle():
                dve.wait_ge(const_step, made[0])

            V = nc.vector
            const(V.memset(ones_bf[:, :], 1.0))
            const(V.memset(ones_f[:, :], 1.0))
            const(V.memset(eps_ln[:, :], EPS_LN))
            const(V.memset(bias_split[:, :, :], 0.0))
            dve.wait_ge(iota_done, 1)
            const(V.tensor_scalar(identity[:, :], iota_p[:, :], 0.0, None, ALU.is_equal))
            const(V.tensor_scalar(before[:, :], iota_p[:, :], 0.0, None, ALU.is_gt))
            dve.wait_ge(loaded_small, 16 * 11)
            const(V.tensor_scalar(w_freq[:, :, :], w_freq_raw[:, :, :], INV_TWO_PI, None, ALU.mult))
            for b in range(NSEQ):
                const(V.tensor_copy(q[:, b, 0:PAD], idc[:, 0:1].broadcast_to([P, PAD])))
            const(V.tensor_scalar(bias_f[:, 0:P // 2], bias_row[:, 0, 0:P // 2], INV_TWO_PI, None, ALU.mult))
            const(V.tensor_scalar(bias_f[:, P // 2:P], bias_row[:, 0, P // 2:P], INV_TWO_PI, 0.25, ALU.mult, ALU.add))
            settle()
            for n in range(3):
                src = bias_f[:, :] if n == 0 else bias_row[:, n, :]
                const(V.tensor_copy(bias_split[0:1, n, :], src))
                settle()
                const(V.tensor_tensor(left[:, 0, :], src, bias_split[0:1, n, :], ALU.subtract))
                settle()
                const(V.tensor_copy(bias_split[32:33, n, :], left[:, 0, :]))
                const(V.tensor_copy(bias_split[96:97, n, :], left[:, 0, :]))
                settle()
                const(V.tensor_scalar(left[:, 1, :], bias_split[32:33, n, :], 0.0, None, ALU.add))
                settle()
                const(V.tensor_tensor(left[:, 1, :], left[:, 0, :], left[:, 1, :], ALU.subtract))
                settle()
                const(V.tensor_copy(bias_split[64:65, n, :], left[:, 1, :]))
                const(V.memset(bias_split[96:97, n, :], 0.0))
            settle()
            V.memset(part[:, :, :], 0.0).then_inc(consts_ready, 1)
            for b in range(NSEQ):
                dve.wait_ge(v0_done, b + 1)
                V.tensor_scalar(vT[:, b, :], Z[b % 2][:, :], b_v[:, 0:1], None, ALU.add).then_inc(v_ready, 1)

            def take_turns(k):
                V.scalar_tensor_tensor(out=turns[:, k, :], in0=turns_rounded[:, k, :], scalar=-MAGIC,
                                       in1=F[k][:, :], op0=ALU.add, op1=ALU.subtract).then_inc(turns_ready, 1)

            def scale(m, k):
                z = Z[k][:, :].rearrange("p (t c) -> p t c", c=C)
                V.tensor_reduce(z_max[:, k, :], z, AX.X, ALU.max, apply_absolute_value=True).then_inc(scale_step, 1)
                dve.wait_ge(scale_step, 3 * m + 1)
                V.tensor_scalar(z_max_eps[:, k, :], z_max[:, k, :], EPS_MAX, None, ALU.add).then_inc(scale_step, 1)
                dve.wait_ge(scale_step, 3 * m + 2)
                V.reciprocal(z_inv[:, k, :], z_max_eps[:, k, :]).then_inc(scale_step, 1)
                dve.wait_ge(scale_step, 3 * m + 3)
                V.tensor_tensor(z_scaled[:, k, :, :], z, z_inv[:, k, :].unsqueeze(2).broadcast_to([P, CH, C]),
                                ALU.mult).then_inc(scaled, 1)

            for b in range(NSEQ):
                dve.wait_ge(rounded, b + 1)
                if b >= 2:
                    dve.wait_ge(waves_ready, b - 1)
                take_turns(b % 2)
                if b >= 1:
                    dve.wait_ge(z_done, b)
                    if b >= 3:
                        dve.wait_ge(turned, b - 2)
                    scale(b - 1, (b - 1) % 2)
            with dve.Fori(1, STEPS) as s:
                for b in range(NSEQ):
                    m = s * NSEQ + b
                    dve.wait_ge(rounded, m + 1)
                    dve.wait_ge(waves_ready, m - 1)
                    take_turns(b % 2)
                    dve.wait_ge(z_done, m)
                    dve.wait_ge(turned, m - 2)
                    scale(m - 1, (b - 1) % 2)
            dve.wait_ge(z_done, ITEMS)
            dve.wait_ge(turned, ITEMS - 2)
            scale(ITEMS - 1, (NSEQ - 1) % 2)

            def gate_q(b):
                dve.wait_ge(q_ready, NSEQ + ITEMS - NSEQ + b + 1)
                if b >= 2:
                    dve.wait_ge(proj_done, b - 1)
                V.tensor_tensor(gated[:, b % 2, :], q[:, b, PAD:PAD + LEN], vT[:, b, :], ALU.mult)\
                    .then_inc(gated_ready, 1)

            dve.wait_ge(loaded_rows, 16)
            gate_q(0)
            for b in range(NSEQ):
                if b + 1 < NSEQ:
                    gate_q(b + 1)
                dve.wait_ge(proj_done, b + 1)
                rows = x1[:, b * CH:(b + 1) * CH, :].rearrange("p t c -> p (t c)")
                V.tensor_tensor(rows, F[b % 2][:, :], rows, ALU.add).then_inc(res_ready, 1)
                dve.wait_ge(res_ready, b + 1)
                for j in range(b * CH, (b + 1) * CH):
                    V.bn_stats(stats[:, j, :], x1[:, j, :]).then_inc(route_step, 1)
                for j in range(b * CH, (b + 1) * CH):
                    dve.wait_ge(route_step, j + 1)
                    V.bn_aggr(mean_var[:, j, :], stats[:, j, :]).then_inc(norm_step, 1)
            dve.wait_ge(std_ready, 1)
            V.reciprocal(rstd[:, :], std[:, :]).then_inc(norm_step, 1)
            dve.wait_ge(norm_step, NT + 1)
            for j in range(NT):
                V.tensor_scalar(x1[:, j, :], x1[:, j, :], mean_var[:, j, 0:1], rstd[:, j:j + 1],
                                ALU.subtract, ALU.mult).then_inc(x1_ready, 1)

            step = [NT]

            def link(ins):
                step[0] += 1
                ins.then_inc(route_step, 1)
                dve.wait_ge(route_step, step[0])

            def over_e(x):
                return x.unsqueeze(2).broadcast_to([P, NT, E])

            dve.wait_ge(logits_done, 1)
            dve.wait_ge(iota_done, 3)
            link(V.tensor_copy(logits[:, :, :], bank[6][:, 0:NT * E].rearrange("p (t e) -> p t e", e=E)))
            link(V.tensor_reduce(col[:, :], logits[:, :, :], AX.X, ALU.max))
            V.tensor_tensor(shifted[:, :, :], logits[:, :, :], over_e(col[:, :]), ALU.subtract).then_inc(shifted_ready, 1)

            def choose(k, values):
                link(V.tensor_tensor(work[:, :, :], values, over_e(col[:, :]), ALU.is_equal))
                link(V.tensor_tensor(work[:, :, :], work[:, :, :], rank_key[:, :, :], ALU.mult))
                link(V.tensor_reduce(col[:, :], work[:, :, :], AX.X, ALU.max))
                link(V.tensor_tensor(pick[k][:, :, :], rank_key[:, :, :], over_e(col[:, :]), ALU.is_equal))

            dve.wait_ge(shifted_ready, 1)
            choose(0, logits[:, :, :])
            link(V.scalar_tensor_tensor(out=masked[:, :, :], in0=pick[0][:, :, :], scalar=NEG,
                                        in1=logits[:, :, :], op0=ALU.mult, op1=ALU.add))
            link(V.tensor_reduce(col[:, :], masked[:, :, :], AX.X, ALU.max))
            choose(1, masked[:, :, :])
            V.tensor_tensor(picked[:, :, :], pick[0][:, :, :], pick[1][:, :, :], ALU.add).then_inc(picked_ready, 1)
            dve.wait_ge(exp_done, 1)
            link(V.tensor_reduce(col[:, :], probs[:, :, :], AX.X, ALU.add))
            link(V.reciprocal(wsum[:, :], col[:, :]))
            link(V.tensor_tensor(probs[:, :, :], probs[:, :, :], over_e(wsum[:, :]), ALU.mult))
            for k in range(TOPK):
                link(V.tensor_tensor(work[:, :, :], probs[:, :, :], pick[k][:, :, :], ALU.mult))
                link(V.tensor_reduce(weight_raw[:, k, :], work[:, :, :], AX.X, ALU.add))
            link(V.tensor_tensor(col[:, :], weight_raw[:, 0, :], weight_raw[:, 1, :], ALU.add))
            link(V.reciprocal(wsum[:, :], col[:, :]))
            for k in range(TOPK):
                link(V.tensor_tensor(weight[:, k, :], weight_raw[:, k, :], wsum[:, :], ALU.mult))
            dve.wait_ge(counts_done, 2)
            link(V.tensor_copy(tile_count[:, :, :], F[0][:, 0:NT * E].rearrange("p (t e) -> p t e", e=E)))
            for e in range(E):
                link(V.tensor_tensor_scan(out=count_to[:, :, e], data0=ones_f[:, 0:NT], data1=tile_count[:, :, e],
                                          initial=0.0, op0=ALU.mult, op1=ALU.add))
            link(V.tensor_scalar(e_tiles[:, :], count_to[:, NT - 1, :], 1.0 / P, (P / 2 - 0.5) / P, ALU.mult, ALU.add))
            link(V.tensor_scalar(e_tiles_r[:, :], e_tiles[:, :], MAGIC, None, ALU.add))
            link(V.tensor_scalar(e_tiles[:, :], e_tiles_r[:, :], -MAGIC, None, ALU.add))
            link(V.tensor_tensor_scan(out=e_end[:, :], data0=ones_f[:, 0:E], data1=e_tiles[:, :], initial=0.0,
                                      op0=ALU.mult, op1=ALU.add))
            link(V.tensor_tensor(e_base[:, :], e_end[:, :], e_tiles[:, :], ALU.subtract))
            link(V.tensor_tensor(place[:, :, :], count_to[:, :, :], tile_count[:, :, :], ALU.subtract))
            link(V.tensor_tensor(place[:, :, :], bank[7][:, 0:NT * E].rearrange("p (t e) -> p t e", e=E),
                                 place[:, :, :], ALU.add))
            link(V.tensor_scalar(e_base[:, :], e_base[:, :], float(P), None, ALU.mult))
            link(V.tensor_tensor(place[:, :, :], place[:, :, :], e_base[:, :].unsqueeze(1).broadcast_to([P, NT, E]),
                                 ALU.add))
            for k in range(TOPK):
                link(V.tensor_tensor(work[:, :, :], place[:, :, :], pick[k][:, :, :], ALU.mult))
                link(V.tensor_reduce(pos_f[:, k, :], work[:, :, :], AX.X, ALU.add))
            link(V.tensor_copy(pos[:, :, :], pos_f[:, :, :]))
            link(V.tensor_tensor(tile_ge[:, :, :], tile_no[:, :, :],
                                 e_end[0:1, :].unsqueeze(1).broadcast_to([1, TILES, E]), ALU.is_ge))
            link(V.tensor_reduce(tile_expert_f[:, :], tile_ge[:, :, :], AX.X, ALU.add))
            V.tensor_scalar(tile_expert[:, :], tile_expert_f[:, :], float(E - 1), None, ALU.min).then_inc(routed, 1)

            def take_cols(k):
                V.tensor_copy(col_tile[:, k, :], bank[6][:, 0:P]).then_inc(col_ready, 1)

            def take_hidden_T():
                V.tensor_copy(hidden_T[:, :, :].rearrange("p a n -> p (a n)"), bank[4][:, :]).then_inc(hidden_T_ready, 1)

            def multiply(k):
                V.tensor_tensor(hidden[:, k, :], bank[2 + k][:, :], act_gate[:, k, :], ALU.mult).then_inc(hidden_ready, 1)

            def slot(i, k):
                if not isinstance(i, int) or i + 1 < TILES:
                    dve.wait_ge(row_turned, i + 2)
                    if not isinstance(i, int) or i >= 1:
                        dve.wait_ge(up_done, i)
                    take_cols(1 - k)
                if not isinstance(i, int) or i >= 1:
                    finish(i - 1)
                dve.wait_ge(act_ready, i + 1)
                dve.wait_ge(up_done, i + 1)
                multiply(k)

            def finish(i):
                dve.wait_ge(hidden_turned, i + 1)
                if not isinstance(i, int) or i >= 1:
                    dve.wait_ge(y_done, i)
                take_hidden_T()

            dve.wait_ge(row_turned, 1)
            take_cols(0)
            for i in range(PEEL):
                slot(i, i % 2)
            with dve.Fori(PEEL // 2, TILES // 2 - 1) as pair:
                for k in range(2):
                    slot(pair * 2 + k, k)
            for i in range(TILES - 2, TILES):
                slot(i, i % 2)
            finish(TILES - 1)

            def add_up(j):
                k = j % 4
                dve.wait_ge(y_fetched[k], 32 * (j // 4 + 1))
                V.scalar_tensor_tensor(out=part[:, j % 2, :], in0=y_back[:, k, 0, :], scalar=weight[:, 0, j:j + 1],
                                       in1=x1[:, j, :], op0=ALU.mult, op1=ALU.add).then_inc(merge_step, 1)
                dve.wait_ge(merge_step, 3 * j + 1)
                V.scalar_tensor_tensor(out=res[:, k, :], in0=y_back[:, k, 1, :], scalar=weight[:, 1, j:j + 1],
                                       in1=part[:, j % 2, :], op0=ALU.mult, op1=ALU.add).then_inc(merge_step, 1)
                dve.wait_ge(merge_step, 3 * j + 2)
                V.bn_stats(stats2[:, j % 2, :], res[:, k, :]).then_inc(merge_step, 1)
                dve.wait_ge(merge_step, 3 * j + 3)
                V.bn_aggr(mean_var2[:, k, :], stats2[:, j % 2, :]).then_inc(var_ready, 1)

            def norm2(j):
                k = j % 4
                dve.wait_ge(std2_ready, j + 1)
                V.reciprocal(rstd2[:, k:k + 1], std2[:, k:k + 1]).then_inc(scale_step, 1)
                dve.wait_ge(scale_step, 3 * ITEMS + j + 1)
                dve.wait_ge(var_ready, j + 1)
                if j >= 4:
                    dve.wait_ge(out_stored[k], 16 * (j // 4))
                V.tensor_scalar(out_tile[:, k, :], res[:, k, :], mean_var2[:, k, 0:1], rstd2[:, k:k + 1],
                                ALU.subtract, ALU.mult).then_inc(out_ready, 1)

            for j in range(NT):
                add_up(j)
                if j >= 1:
                    norm2(j - 1)
            norm2(NT - 1)


def kernel(**inputs):
    import numpy as np
    import concourse.bacc as bacc
    from concourse.bass_utils import run_bass_kernel_spmd

    a = {k: np.asarray(v) for k, v in inputs.items()}
    x = a["L0_attn_x"].reshape(NT * P, C)
    fw = a["L0_attn_freq_W"].reshape(2, C, P // 2)
    fb = a["L0_attn_freq_b"]
    host = {
        "x_rows": x.reshape(NT, P, C).transpose(1, 0, 2),
        "x_cols": x.T,
        "attn_W": a["L0_attn_attn_W"],
        "attn_bq": a["L0_attn_attn_b"][:C].reshape(C, 1),
        "attn_bv": a["L0_attn_attn_b"][C:].reshape(C, 1),
        "freq_W": np.concatenate([fw, fw], axis=2).transpose(1, 0, 2),
        "freq_b": np.concatenate([fb, fb]).reshape(1, P),
        "out_W": a["L0_attn_out_W"],
        "out_b": a["L0_attn_out_b"].reshape(1, C),
        "proj_W": a["L0_attn_proj_W"],
        "proj_b": a["L0_attn_proj_b"].reshape(1, C),
        "ident_col": a["L0_attn_identity"].reshape(C, 1),
        "gate_T": a["L0_ffn_gate_w"].T,
        "gu_T": a["L0_ffn_gate_up_proj"].transpose(2, 0, 1),
        "dn_T": a["L0_ffn_down_proj"].transpose(0, 2, 1).reshape(E, HC, P, C).transpose(2, 0, 1, 3),
    }
    nc = bacc.Bacc("TRN2", target_bir_lowering=False, num_devices=1)
    arrays, args = {}, []
    for name, v in host.items():
        v = np.ascontiguousarray(v)
        arrays[name] = v
        args.append(nc.dram_tensor(name, v.shape, mybir.dt.from_np(v.dtype), kind="ExternalInput").ap())
    out = nc.dram_tensor("out_rows", (NT * P, C), F32, kind="ExternalOutput").ap()
    build(nc, *args, out)
    r = run_bass_kernel_spmd(nc, [arrays], core_ids=[0])
    return r.results[0]["out_rows"].reshape(NSEQ, LEN, C)
```

```python
from contextlib import ExitStack

import concourse.bass as bass
from concourse import mybir

ALU = mybir.AluOpType
ACT = mybir.ActivationFunctionType
AX = mybir.AxisListType
F32 = mybir.dt.float32
F16 = mybir.dt.float16
BF16 = mybir.dt.bfloat16
I32 = mybir.dt.int32
U32 = mybir.dt.uint32

P = 128
NSEQ, LEN, C = 8, 512, 128
STEPS = 9
PAD = LEN // 2
CH = LEN // P
NT = NSEQ * CH
GROUPS = 2
SG, NTG = NSEQ // GROUPS, NT // GROUPS
E, HID = 8, 512
HC = HID // P
TOPK = 2
TG = NTG * TOPK + E
TILES = GROUPS * TG
ROW = C + 2
ITEMS = STEPS * SG
QUADS = TILES // 4
PARTS = 21
PART_STEPS = 6
PART_QUADS = 6
X_SCALE = 2.0 ** 10
W_TOP = 2.0 ** 14
EPS_MAX, EPS_LN = 1e-6, 1e-5
MAGIC = 1.5 * 2.0 ** 23
INV_TWO_PI = 0.15915494309189535
TWO_PI = 6.2831850
NEG = -3.0e38


def build(nc, x_rows, x_cols, attn_W, attn_bq, attn_bv, freq_W, freq_b, out_W, out_b, proj_W, proj_b,
          ident_col, gate_T, gu_T, dn_T, out):
    ctx = ExitStack()
    with ctx:
        def sb(name, shape, dt=F32):
            return ctx.enter_context(nc.sbuf_tensor(name, shape, dt))

        def ps(name, shape, dt=F32):
            return ctx.enter_context(nc.psum_tensor(name, shape, dt))

        def sem(name):
            return ctx.enter_context(nc.semaphore(name))

        w_attn = sb("w_attn", [P, 2 * C])
        b_q = sb("b_q", [P, 1])
        b_v = sb("b_v", [P, 1])
        w_freq_raw = sb("w_freq_raw", [P, 2, P])
        w_freq = sb("w_freq", [P, 2, P])
        w_out = sb("w_out", [P, C])
        w_proj = sb("w_proj", [P, C])
        w_gate = sb("w_gate", [P, E])
        w_raw = sb("w_raw", [P, E, 2 * HID])
        w_high = sb("w_high", [P, E, 2 * HID], F16)
        w_low = sb("w_low", [P, E, 2 * HID], F16)
        w_max_e = sb("w_max_e", [P, E])
        w_max = sb("w_max", [P, 1])
        w_max_all = sb("w_max_all", [P, 1])
        w_power = sb("w_power", [P, 1])
        w_inv = sb("w_inv", [P, 1])
        w_scale = sb("w_scale", [P, 1])
        unscale = sb("unscale", [P, 1])
        w_dn = sb("w_dn", [P, E, HC, C])
        bias_row = sb("bias_row", [1, 3, P])
        bias_f = sb("bias_f", [1, P])
        left = sb("left", [1, 2, P])
        bias_split = sb("bias_split", [P, 3, P], BF16)
        ones_bf = sb("ones_bf", [P, LEN], BF16)
        iota_p = sb("iota_p", [P, P])
        identity = sb("identity", [P, P])
        identity_h = sb("identity_h", [P, P], F16)
        before = sb("before", [P, P], BF16)
        idc = sb("idc", [P, 1])
        xT = sb("xT", [P, NT, P])
        x1 = sb("x1", [P, NT, C])
        q = sb("q", [P, NSEQ, PAD + LEN])
        turns_rounded = sb("turns_rounded", [P, 2, LEN])
        turns = sb("turns", [P, 2, LEN])
        waves = sb("waves", [P, 2, LEN])
        z_scaled = sb("z_scaled", [P, 2, CH, C])
        z_max = sb("z_max", [P, 2, CH])
        z_max_eps = sb("z_max_eps", [P, 2, CH])
        z_inv = sb("z_inv", [P, 2, CH])
        x1T = sb("x1T", [P, 2, LEN])
        gated = sb("gated", [P, 2, LEN])
        stats = sb("stats", [P, NT, 6])
        mean_var = sb("mean_var", [P, NT, 2])
        std = sb("std", [P, NT])
        rstd = sb("rstd", [P, NT])
        logits = sb("logits", [P, NTG, E])
        shifted = sb("shifted", [P, NTG, E])
        probs = sb("probs", [P, NTG, E])
        rank_key = sb("rank_key", [P, NTG, E])
        work = sb("work", [P, NTG, E])
        pick = [sb(f"pick{k}", [P, NTG, E]) for k in range(TOPK)]
        masked = sb("masked", [P, NTG, E])
        picked = sb("picked", [P, NTG, E], BF16)
        col = sb("col", [P, NTG])
        weight_raw = sb("weight_raw", [P, TOPK, NTG])
        wsum = sb("wsum", [P, NTG])
        tile_count = sb("tile_count", [P, NTG, E])
        ones_f = sb("ones_f", [P, NT])
        count_to = sb("count_to", [P, NTG, E])
        place = sb("place", [P, NTG, E])
        e_tiles = sb("e_tiles", [P, E])
        e_tiles_r = sb("e_tiles_r", [P, E])
        e_end = sb("e_end", [P, E])
        e_base = sb("e_base", [P, E])
        pos_f = sb("pos_f", [P, TOPK, NT])
        pos = sb("pos", [P, TOPK, NT], U32)
        tile_no = sb("tile_no", [1, TG, E])
        tile_ge = sb("tile_ge", [1, TG, E])
        tile_expert_f = sb("tile_expert_f", [1, TG])
        tile_at = sb("tile_at", [1, 1 + TILES], I32)
        send = sb("send", [P, NTG, TOPK, ROW])
        target = sb("target", [P, NT, TOPK], U32)
        row_tile = sb("row_tile", [P, 2, ROW])
        meta = sb("meta", [P, 4, 2])
        col_tile = sb("col_tile", [P, 2, 2, P], F16)
        act_gate = turns_rounded
        hidden = turns
        y_tile = sb("y_tile", [P, 4, C])
        y_back = waves[:, :, :].rearrange("p n (t k c) -> p n t k c", t=2, k=TOPK)
        y_sum = z_scaled[:, :, 0:2, :]
        stats2 = sb("stats2", [P, NT, 6])
        mean_var2 = sb("mean_var2", [P, NT, 2])
        std2 = sb("std2", [P, NT])
        rstd2 = sb("rstd2", [P, NT])
        eps_ln = sb("eps_ln", [P, 1])

        bank = [ps(f"bank{i}", [P, LEN]) for i in range(8)]
        F, Z, T = bank[0:2], bank[2:4], bank[4:6]

        sorted_x = nc.dram_tensor("sorted_x", [TILES * P, ROW], F32, kind="Internal").ap()
        y_tok = nc.dram_tensor("y_tok", [NT * P * TOPK + TILES * P, C], F32, kind="Internal").ap()

        loaded_small = sem("loaded_small")
        loaded_xT = sem("loaded_xT")
        loaded_rows = sem("loaded_rows")
        loaded_experts = sem("loaded_experts")
        iota_done = sem("iota_done")
        const_step = sem("const_step")
        consts_ready = sem("consts_ready")
        blank_ready = sem("blank_ready")
        filled = sem("filled")
        max_ready = sem("max_ready")
        max_all = sem("max_all")
        scale_ready = sem("scale_ready")
        w_step = sem("w_step")
        high_ready = sem("high_ready")
        low_ready = sem("low_ready")
        high_sent = sem("high_sent")
        q0_done = sem("q0_done")
        v_done = sem("v_done")
        q_ready = sem("q_ready")
        f_done = sem("f_done")
        rounded = sem("rounded")
        turns_ready = sem("turns_ready")
        waves_ready = sem("waves_ready")
        z_done = sem("z_done")
        scale_step = sem("scale_step")
        scaled = sem("scaled")
        turned = sem("turned")
        gated_ready = sem("gated_ready")
        proj_done = sem("proj_done")
        res_ready = sem("res_ready")
        norm_step = sem("norm_step")
        std_ready = sem("std_ready")
        x1_ready = sem("x1_ready")
        x1T_done = sem("x1T_done")
        x1T_ready = sem("x1T_ready")
        route_step = sem("route_step")
        exp_done = sem("exp_done")
        counts_done = sem("counts_done")
        picked_ready = sem("picked_ready")
        shifted_ready = sem("shifted_ready")
        routed = sem("routed")
        sent = sem("sent")
        row_loaded = [sem(f"row_loaded{k}") for k in range(2)]
        row_turned = sem("row_turned")
        col_ready = sem("col_ready")
        gate_done = sem("gate_done")
        up_done = sem("up_done")
        act_ready = sem("act_ready")
        hidden_ready = sem("hidden_ready")
        meta_ready = sem("meta_ready")
        y_done = sem("y_done")
        y_ready = sem("y_ready")
        y_stored = [sem(f"y_stored{k}") for k in range(4)]
        y_fetched = [sem(f"y_fetched{k}") for k in range(2)]
        y_summed = sem("y_summed")
        merged = sem("merged")
        stats2_ready = sem("stats2_ready")
        var_ready = sem("var_ready")
        std2_ready = sem("std2_ready")
        rstd2_ready = sem("rstd2_ready")
        out_ready = sem("out_ready")
        out_stored = sem("out_stored")
        send_step = sem("send_step")
        rows_ready = sem("rows_ready")
        moved = sem("moved")
        y_taken = sem("y_taken")
        target_ready = sem("target_ready")
        rows_step = sem("rows_step")
        scan_step = sem("scan_step")
        stats_step = sem("stats_step")
        gate_read = sem("gate_read")

        block = ctx.enter_context(nc.Block())
        SMALL = 12

        @block.sync
        def _(sp):
            for dst, src in ((w_attn[:, :], attn_W), (b_q[:, :], attn_bq), (b_v[:, :], attn_bv),
                             (w_freq_raw[:, :, :], freq_W), (w_out[:, :], out_W), (w_proj[:, :], proj_W),
                             (w_gate[:, :], gate_T), (bias_row[:, 0, :], freq_b), (bias_row[:, 1, :], out_b),
                             (bias_row[:, 2, :], proj_b), (idc[:, :], ident_col)):
                sp.dma_start(dst, src).then_inc(loaded_small, 16)
            sp.dma_start(xT[:, :, :], x_cols.rearrange("c (t p) -> c t p", p=P)).then_inc(loaded_xT, 16)
            sp.dma_start(x1[:, :, :], x_rows).then_inc(loaded_rows, 16)
            sp.dma_start(w_raw[:, :, :], gu_T).then_inc(loaded_experts, 16)
            sp.dma_start(w_dn[:, :, :, :], dn_T).then_inc(loaded_experts, 16)

            def load_rows(i, k):
                if not isinstance(i, int) or i >= 2:
                    sp.wait_ge(row_turned, i - 1)
                    sp.wait_ge(meta_ready, i - 1)
                sp.dma_start(row_tile[:, k, :], sorted_x[bass.ds(i * P, P), :]).then_inc(row_loaded[k], 16)

            def load_y(pair, k, half):
                if half:
                    sp.wait_ge(y_summed, pair - 1)
                sp.dma_start(y_back[:, k, :, :, :],
                             y_tok[bass.ds(pair * 2 * P * TOPK, 2 * P * TOPK), :].rearrange(
                                 "(t p k) c -> p t k c", p=P, k=TOPK)).then_inc(y_fetched[k], 16)

            sp.wait_ge(sent, 16 * TOPK * NTG)
            for i in range(4):
                load_rows(i, i % 2)
            with sp.Fori(1, TG // 4) as quad:
                for r in range(4):
                    load_rows(quad * 4 + r, r % 2)
            sp.wait_ge(sent, 16 * TOPK * NT)
            with sp.Fori(TG // 4, TG // 4 + 2) as quad:
                for r in range(4):
                    load_rows(quad * 4 + r, r % 2)
            for r in range(4):
                sp.wait_ge(y_stored[r], 16 * (TG // 4))
            load_y(0, 0, False)
            load_y(1, 1, False)
            for r in range(4):
                load_rows((TG // 4 + 2) * 4 + r, r % 2)
            for r in range(4):
                load_rows((TG // 4 + 3) * 4 + r, r % 2)
            with sp.Fori(1, NTG // 4) as n:
                for k in range(2):
                    load_y(n * 2 + k, k, True)
                    for r in range(4):
                        load_rows((n * 2 + (k + TG // 4 + 2)) * 4 + r, r % 2)
            for r in range(4):
                sp.wait_ge(y_stored[r], 16 * QUADS)
            for pair in range(NTG // 2, NT // 2):
                load_y(pair, pair % 2, True)
            for b in range(NSEQ):
                sp.wait_ge(out_ready, (b + 1) * CH)
                sp.dma_start(out[b * LEN:(b + 1) * LEN, :].rearrange("(t p) c -> p t c", p=P),
                             x1[:, b * CH:(b + 1) * CH, :]).then_inc(out_stored, 16)
            sp.wait_ge(out_stored, 16 * NSEQ)

        @block.gpsimd
        def _(pool):
            nc.gpsimd.iota(iota_p[:, :], pattern=[[1, P]], base=0, channel_multiplier=-1,
                           allow_small_or_imprecise_dtypes=True).then_inc(iota_done, 1)
            nc.gpsimd.iota(tile_no[:, :, :], pattern=[[1, TG], [0, E]], base=0, channel_multiplier=0,
                           allow_small_or_imprecise_dtypes=True).then_inc(iota_done, 1)
            nc.gpsimd.iota(rank_key[:, :, :], pattern=[[0, NTG], [-1, E]], base=E, channel_multiplier=0,
                           allow_small_or_imprecise_dtypes=True).then_inc(iota_done, 1)
            nc.gpsimd.iota(target[:, :, :], pattern=[[P * TOPK, NT], [1, TOPK]], base=0,
                           channel_multiplier=TOPK).then_inc(target_ready, 1)
            pool.wait_ge(blank_ready, 1)
            slots = send[:, :, :, :].rearrange("p t k c -> p (t k) c")
            at, n = 0, 0
            while at < TILES:
                wide = min(NTG * TOPK, TILES - at)
                if n:
                    pool.wait_ge(filled, 16 * n)
                nc.gpsimd.iota(slots[:, 0:wide, C + 1:C + 2].bitcast(U32), pattern=[[P, wide], [0, 1]],
                               base=NT * P * TOPK + at * P, channel_multiplier=1).then_inc(send_step, 1)
                pool.wait_ge(send_step, n + 1)
                pool.dma_start(sorted_x[at * P:(at + wide) * P, :].rearrange("(t p) c -> p t c", p=P),
                               slots[:, 0:wide, :]).then_inc(filled, 16)
                at += wide
                n += 1
            pool.wait_ge(filled, 16 * n)

            pool.wait_ge(max_ready, 1)
            nc.gpsimd.partition_all_reduce(w_max_all[:, :], w_max[:, :], P, bass.bass_isa.ReduceOp.max)\
                .then_inc(max_all, 1)

            def send_rows(j, k):
                nc.gpsimd.indirect_dma_start(
                    out=sorted_x, out_offset=bass.IndirectOffsetOnAxis(ap=pos[:, k, j:j + 1], axis=0),
                    in_=send[:, j % NTG, k, :], in_offset=None).then_inc(sent, 16)

            def store_y(r):
                nc.gpsimd.indirect_dma_start(
                    out=y_tok, out_offset=bass.IndirectOffsetOnAxis(ap=meta[:, r, 1:2].bitcast(U32), axis=0),
                    in_=y_tile[:, r, :], in_offset=None).then_inc(y_stored[r], 16)

            for e in range(E):
                pool.wait_ge(high_ready, 2 * (e + 1))
                nc.gpsimd.tensor_tensor(w_low[:, e, :], w_raw[:, e, :], w_high[:, e, :], ALU.subtract)\
                    .then_inc(low_ready, 1)
            pool.wait_ge(rows_ready, 1)
            for j in range(NTG):
                for k in range(TOPK):
                    send_rows(j, k)
            for i in range(TG):
                n = i - PARTS + 1
                if n == 0:
                    pool.wait_ge(rows_ready, 2)
                if 0 <= n < NTG:
                    for k in range(TOPK):
                        send_rows(NTG + n, k)
                pool.wait_ge(y_ready, i + 1)
                store_y(i % 4)
            with pool.Fori(TG // 4, QUADS) as quad:
                for r in range(4):
                    pool.wait_ge(y_ready, quad * 4 + (r + 1))
                    pool.sem_inc(y_taken, 1)
                    store_y(r)

        @block.tensor
        def _(pe):
            pe.wait_ge(loaded_small, 16 * 11)
            pe.wait_ge(loaded_xT, 16)
            for b in range(NSEQ):
                if b >= 2:
                    pe.wait_ge(q_ready, b - 1)
                nc.tensor.matmul(F[b % 2][:, :], w_attn[:, 0:C], xT[:, b * CH:(b + 1) * CH, :],
                                 start=True, stop=True).then_inc(q0_done, 1)
            pe.wait_ge(q_ready, NSEQ)
            pe.wait_ge(consts_ready, 1)

            def angles(b, shift):
                k = b % 2
                nc.tensor.matmul(F[k][:, :], bias_split[:, 0, :], ones_bf[:, :], start=True, stop=False)
                nc.tensor.matmul(F[k][:, :], w_freq[:, 0, :], q[:, b, bass.ds(PAD - shift, LEN)], start=False, stop=False)
                nc.tensor.matmul(F[k][:, :], w_freq[:, 1, :], q[:, b, PAD:PAD + LEN],
                                 start=False, stop=True).then_inc(f_done, 1)

            def mix(b):
                k = b % 2
                nc.tensor.matmul(Z[k][:, :], ones_bf[:, 0:P], bias_split[:, 1:2, :].broadcast_to([P, CH, P]),
                                 start=True, stop=False, skip_group_check=True)
                for c in range(CH):
                    last = nc.tensor.matmul(Z[k][:, c * P:(c + 1) * P], waves[:, k, c * P:(c + 1) * P], w_out[:, :],
                                            start=False, stop=(c == CH - 1), skip_group_check=True)
                last.then_inc(z_done, 1)

            def turn(b):
                k = b % 2
                for c in range(CH):
                    last = nc.tensor.transpose(T[k][:, c * P:(c + 1) * P], z_scaled[:, k, c, :], identity[:, :])
                last.then_inc(turned, 1)

            def values(b):
                if b % SG:
                    pe.wait_ge(gated_ready, b)
                elif b:
                    pe.wait_ge(routed, b // SG)
                nc.tensor.matmul(bank[6][:, :], w_attn[:, C:2 * C], xT[:, b * CH:(b + 1) * CH, :],
                                 start=True, stop=True).then_inc(v_done, 1)

            def project(b):
                pe.wait_ge(gated_ready, b + 1)
                if b % SG:
                    pe.wait_ge(res_ready, b)
                nc.tensor.matmul(bank[7][:, :], ones_bf[:, 0:P], bias_split[:, 2:3, :].broadcast_to([P, CH, P]),
                                 start=True, stop=False, skip_group_check=True)
                for c in range(CH):
                    last = nc.tensor.matmul(bank[7][:, c * P:(c + 1) * P], gated[:, b % 2, c * P:(c + 1) * P],
                                            w_proj[:, :], start=False, stop=(c == CH - 1), skip_group_check=True)
                last.then_inc(proj_done, 1)

            def turn_x1(b):
                pe.wait_ge(x1_ready, (b + 1) * CH)
                if b % SG:
                    pe.wait_ge(x1T_ready, b)
                for c in range(CH):
                    last = nc.tensor.transpose(bank[6][:, c * P:(c + 1) * P], x1[:, b * CH + c, :], identity[:, :])
                last.then_inc(x1T_done, 1)

            def gate(b):
                pe.wait_ge(x1T_ready, b + 1)
                if b % SG == 0:
                    pe.wait_ge(res_ready, b + SG)
                for c in range(CH):
                    j = b % SG * CH + c
                    last = nc.tensor.matmul(bank[7][:, j * E:(j + 1) * E], x1T[:, b % 2, c * P:(c + 1) * P], w_gate[:, :],
                                            start=True, stop=True, skip_group_check=True)
                last.then_inc(gate_read, 1)

            def norm_and_route(g, n):
                if n < 2 * SG:
                    (values, project)[n % 2](g * SG + n // 2)
                if 2 * SG + 2 <= n < 3 * SG + 2:
                    gate(g * SG + n - 2 * SG - 2)
                if 2 * SG + 1 <= n < 3 * SG + 1:
                    turn_x1(g * SG + n - 2 * SG - 1)
                if n == 16:
                    pe.wait_ge(picked_ready, g + 1)
                    pe.wait_ge(x1T_ready, (g + 1) * SG)
                    nc.tensor.matmul(bank[6][:, 0:NTG * E], before[:, :], picked[:, :, :], start=True, stop=True,
                                     skip_group_check=True).then_inc(counts_done, 1)
                    nc.tensor.matmul(bank[6][:, NTG * E:2 * NTG * E], ones_bf[:, 0:P], picked[:, :, :], start=True,
                                     stop=True, skip_group_check=True).then_inc(counts_done, 1)

            def scan(g):
                first = g * ITEMS
                b0 = g * SG
                for b in range(SG):
                    m = first + b
                    if m >= 2:
                        pe.wait_ge(turns_ready, m - 1)
                    angles(b0 + b, 1)
                    if b >= 1:
                        pe.wait_ge(waves_ready, m)
                        if m >= 3:
                            pe.wait_ge(scaled, m - 2)
                        mix(b0 + b - 1)
                    if b >= 2:
                        pe.wait_ge(scaled, m - 1)
                        if m >= 4:
                            pe.wait_ge(q_ready, NSEQ + m - 3)
                        turn(b0 + b - 2)
                def item(s, b):
                    m = s * SG + (first + b)
                    pe.wait_ge(q_ready, m + (NSEQ - SG + 1))
                    pe.wait_ge(turns_ready, m - 1)
                    angles(b0 + b, 1 << s)
                    pe.wait_ge(waves_ready, m)
                    pe.wait_ge(scaled, m - 2)
                    mix(b0 + (b - 1) % SG)
                    pe.wait_ge(scaled, m - 1)
                    pe.wait_ge(q_ready, m + (NSEQ - 3))
                    turn(b0 + (b - 2) % SG)

                looped = 1
                if g:
                    for s in range(1, 1 + PART_STEPS):
                        for b in range(SG):
                            item(s, b)
                            norm_and_route(g - 1, (s - 1) * SG + b)
                    looped += PART_STEPS
                with pe.Fori(looped, STEPS) as s:
                    for b in range(SG):
                        item(s, b)
                end = first + ITEMS
                pe.wait_ge(waves_ready, end)
                pe.wait_ge(scaled, end - 2)
                mix(b0 + SG - 1)
                for m in (end - 2, end - 1):
                    pe.wait_ge(scaled, m + 1)
                    pe.wait_ge(q_ready, NSEQ + m - 1)
                    turn(b0 + SG - (end - m))

            for g in range(GROUPS):
                scan(g)

            pe.wait_ge(routed, 1)
            pe.wait_ge(loaded_experts, 32)
            pe.wait_ge(high_ready, 2 * E)
            pe.wait_ge(low_ready, E)

            def turn_rows(i, k):
                pe.wait_ge(row_loaded[k], (i // 2 + 1) * 16 if isinstance(i, int) else (i - k) * 8 + 16)
                if not isinstance(i, int) or i >= 1:
                    pe.wait_ge(col_ready, i)
                halves = row_tile[:, k, 0:C].bitcast(F16)
                to = bank[4][:, 0:P].bitcast(F16)
                nc.tensor.transpose(to[:, 0:P], halves[:, 0:P], identity_h[:, :])
                nc.tensor.transpose(to[:, P:2 * P], halves[:, P:2 * P], identity_h[:, :]).then_inc(row_turned, 1)

            def gate_up(k, at, half):
                for c in range(HC):
                    to = bank[2 * half + k][:, c * P:(c + 1) * P]
                    here = bass.ds(at + (half * HID + c * P), P)
                    nc.tensor.matmul(to, highs[:, here], col_tile[:, k, 1, :], start=True, stop=False,
                                     skip_group_check=True)
                    nc.tensor.matmul(to, highs[:, here], col_tile[:, k, 0, :], start=False, stop=False,
                                     skip_group_check=True)
                    last = nc.tensor.matmul(to, lows[:, here], col_tile[:, k, 0, :], start=False, stop=True,
                                            skip_group_check=True)
                last.then_inc((gate_done, up_done)[half], 1)

            def down(i, k, at):
                pe.wait_ge(hidden_ready, i + 1)
                if not isinstance(i, int) or i >= 1:
                    pe.wait_ge(y_ready, i)
                for c in range(HC):
                    last = nc.tensor.matmul(bank[5][:, 0:C], hidden[:, k, c * P:(c + 1) * P],
                                            downs[:, bass.ds(at + c * C, C)],
                                            start=(c == 0), stop=(c == HC - 1))
                last.then_inc(y_done, 1)

            highs = w_high[:, :, :].rearrange("p e n -> p (e n)")
            lows = w_low[:, :, :].rearrange("p e n -> p (e n)")
            downs = w_dn[:, :, :, :].rearrange("p e a n -> p (e a n)")
            places = [pe.alloc_register(f"place{n}") for n in range(5)]

            def load_places(quad):
                pe.reg_load(places, tile_at[0:1, bass.ds(quad * 4, 5)])

            def quad_slots(quad):
                at = [pe.snap(x, min_val=0, max_val=(E - 1) * HC * C, out_of_modulus=HC * C) for x in places]
                for r in range(4):
                    i, k = quad * 4 + r, r % 2
                    if not isinstance(i, int) or i + 1 < TILES:
                        turn_rows(i + 1, 1 - k)
                    up_at = pe.snap(at[r + 1] * 2)
                    pe.wait_ge(col_ready, i + 1)
                    if not isinstance(i, int) or i >= 2:
                        pe.wait_ge(act_ready, i - 1)
                    gate_up(k, up_at, 0)
                    if not isinstance(i, int) or i >= 2:
                        pe.wait_ge(hidden_ready, i - 1)
                    gate_up(k, up_at, 1)
                    if r == 3 and not (isinstance(i, int) and i == TILES - 1):
                        load_places(quad + 1)
                    if not isinstance(i, int) or i >= 1:
                        down(i - 1, 1 - k, at[r])
                    if isinstance(i, int) and i < PARTS:
                        norm_and_route(1, i)
                return at[4]

            pe.wait_ge(q_ready, NSEQ + GROUPS * ITEMS)
            load_places(0)
            turn_rows(0, 0)
            for quad in range(PART_QUADS):
                quad_slots(quad)
            pe.wait_ge(routed, GROUPS)
            with pe.Fori(PART_QUADS, QUADS - 1) as quad:
                quad_slots(quad)
            last_at = quad_slots(QUADS - 1)
            down(TILES - 1, 1, last_at)

        @block.scalar
        def _(act):
            act.wait_ge(loaded_small, 16 * 11)
            for b in range(NSEQ):
                act.wait_ge(q0_done, b + 1)
                nc.scalar.activation(q[:, b, PAD:PAD + LEN], F[b % 2][:, :], ACT.Identity,
                                     bias=b_q[:, 0:1]).then_inc(q_ready, 1)

            def round_turns(k):
                nc.scalar.activation(turns_rounded[:, k, :], F[k][:, :], ACT.Copy, bias=MAGIC).then_inc(rounded, 1)

            def wave(k):
                nc.scalar.activation(waves[:, k, :], turns[:, k, :], ACT.Sin, scale=-TWO_PI).then_inc(waves_ready, 1)

            def take_q(b):
                nc.scalar.activation(q[:, b, PAD:PAD + LEN], T[b % 2][:, :], ACT.Copy).then_inc(q_ready, 1)

            def split_weights(e, whole):
                if whole:
                    act.wait_ge(high_ready, 2 * e + 1)
                elif e == 0:
                    act.wait_ge(scale_ready, 1)
                nc.scalar.activation((w_raw if whole else w_high)[:, e, :], w_raw[:, e, :], ACT.Copy,
                                     scale=w_scale[:, 0:1]).then_inc(high_ready, 1)

            def norm_and_route(g, n):
                t0, t1 = g * NTG, (g + 1) * NTG
                if n == 8:
                    act.wait_ge(norm_step, t1 + g)
                    nc.scalar.activation(std[:, t0:t1], mean_var[:, t0:t1, 1], ACT.Sqrt, bias=eps_ln[:, 0:1])\
                        .then_inc(std_ready, 1)
                if 2 * SG + 1 <= n < 3 * SG + 1:
                    b = g * SG + n - 2 * SG - 1
                    act.wait_ge(x1T_done, b + 1)
                    if b >= 2:
                        act.wait_ge(gate_read, b - 1)
                    nc.scalar.activation(x1T[:, b % 2, :], bank[6][:, :], ACT.Copy).then_inc(x1T_ready, 1)
                if n in (12, 13):
                    if n == 12:
                        act.wait_ge(filled if g == 0 else sent, 16 * 3 if g == 0 else 16 * TOPK * NTG)
                        act.wait_ge(x1_ready, t1)
                    nc.scalar.activation(send[:, :, n - 12, 0:C // 2].bitcast(F16), x1[:, t0:t1, :], ACT.Copy,
                                         scale=X_SCALE).then_inc(high_sent, 1)
                if n == 14:
                    act.wait_ge(moved, 2 * g + 1)
                    nc.scalar.activation(send[:, :, 1, C // 2:C].bitcast(F16), send[:, :, 0, C // 2:C].bitcast(F16),
                                         ACT.Copy).then_inc(rows_step, 1)
                if n == 15:
                    act.wait_ge(shifted_ready, g + 1)
                    nc.scalar.activation(probs[:, :, :], shifted[:, :, :], ACT.Exp).then_inc(exp_done, 1)

            def scan(g):
                first = g * ITEMS
                b0 = g * SG
                for b in range(SG):
                    m = first + b
                    act.wait_ge(f_done, m + 1)
                    if m >= 2:
                        act.wait_ge(turns_ready, m - 1)
                    round_turns(b % 2)
                    if b >= 2:
                        act.wait_ge(turned, m - 1)
                        take_q(b0 + b - 2)
                    act.wait_ge(turns_ready, m + 1)
                    if m >= 2:
                        act.wait_ge(z_done, m - 1)
                    wave(b % 2)

                def item(s, b):
                    m = s * SG + (first + b)
                    act.wait_ge(f_done, m + 1)
                    act.wait_ge(turns_ready, m - 1)
                    round_turns(b % 2)
                    act.wait_ge(turned, m - 1)
                    take_q(b0 + (b - 2) % SG)
                    act.wait_ge(turns_ready, m + 1)
                    act.wait_ge(z_done, m - 1)
                    wave(b % 2)

                looped = 1
                if g:
                    for s in range(1, 1 + PART_STEPS):
                        for b in range(SG):
                            item(s, b)
                            n = (s - 1) * SG + b
                            norm_and_route(g - 1, n)
                            if 1 <= n < 1 + 2 * E:
                                split_weights((n - 1) // 2, (n - 1) % 2)
                    looped += PART_STEPS
                with act.Fori(looped, STEPS) as s:
                    for b in range(SG):
                        item(s, b)
                for m in (first + ITEMS - 2, first + ITEMS - 1):
                    act.wait_ge(turned, m + 1)
                    take_q(b0 + SG - (first + ITEMS - m))

            for g in range(GROUPS):
                scan(g)

            def silu(k):
                nc.scalar.activation(act_gate[:, k, :], bank[k][:, :], ACT.Silu, scale=unscale[:, 0:1])\
                    .then_inc(act_ready, 1)

            def take_y(i, r, again):
                act.wait_ge(y_done, i + 1)
                act.wait_ge(meta_ready, i + 1)
                if not isinstance(again, int) or again >= 1:
                    act.wait_ge(y_stored[r], again * 16)
                nc.scalar.activation(y_tile[:, r, :], bank[5][:, 0:C], ACT.Copy,
                                     scale=meta[:, r, 0:1]).then_inc(y_ready, 1)

            def slot(quad, r):
                i = quad * 4 + r
                act.wait_ge(gate_done, i + 1)
                if not isinstance(i, int) or i >= 2:
                    act.wait_ge(hidden_ready, i - 1)
                silu(r % 2)
                if not isinstance(i, int) or i >= 1:
                    take_y(i - 1, (r - 1) % 4, quad if r else quad - 1)
                if isinstance(i, int) and i < PARTS:
                    norm_and_route(1, i)

            act.wait_ge(scale_ready, 1)
            for quad in range(PART_QUADS):
                for r in range(4):
                    slot(quad, r)
            with act.Fori(PART_QUADS, QUADS) as quad:
                for r in range(4):
                    slot(quad, r)
            take_y(TILES - 1, 3, QUADS - 1)

            act.wait_ge(var_ready, NT)
            nc.scalar.activation(std2[:, :], mean_var2[:, :, 1], ACT.Sqrt, bias=eps_ln[:, 0:1]).then_inc(std2_ready, 1)

        @block.vector
        def _(dve):
            made = [0]

            def const(ins):
                made[0] += 1
                ins.then_inc(const_step, 1)

            def settle():
                dve.wait_ge(const_step, made[0])

            V = nc.vector
            V.memset(send[:, :, :, :], 0.0).then_inc(blank_ready, 1)
            const(V.memset(ones_bf[:, :], 1.0))
            const(V.memset(ones_f[:, :], 1.0))
            const(V.memset(eps_ln[:, :], EPS_LN))
            const(V.memset(bias_split[:, :, :], 0.0))
            dve.wait_ge(iota_done, 1)
            const(V.tensor_scalar(identity[:, :], iota_p[:, :], 0.0, None, ALU.is_equal))
            const(V.tensor_scalar(identity_h[:, :], iota_p[:, :], 0.0, None, ALU.is_equal))
            const(V.tensor_scalar(before[:, :], iota_p[:, :], 0.0, None, ALU.is_gt))
            dve.wait_ge(loaded_small, 16 * 11)
            const(V.tensor_scalar(w_freq[:, :, :], w_freq_raw[:, :, :], INV_TWO_PI, None, ALU.mult))
            for b in range(NSEQ):
                const(V.tensor_copy(q[:, b, 0:PAD], idc[:, 0:1].broadcast_to([P, PAD])))
            const(V.tensor_scalar(bias_f[:, 0:P // 2], bias_row[:, 0, 0:P // 2], INV_TWO_PI, None, ALU.mult))
            const(V.tensor_scalar(bias_f[:, P // 2:P], bias_row[:, 0, P // 2:P], INV_TWO_PI, 0.25, ALU.mult, ALU.add))
            settle()
            for n in range(3):
                src = bias_f[:, :] if n == 0 else bias_row[:, n, :]
                const(V.tensor_copy(bias_split[0:1, n, :], src))
                settle()
                const(V.tensor_tensor(left[:, 0, :], src, bias_split[0:1, n, :], ALU.subtract))
                settle()
                const(V.tensor_copy(bias_split[32:33, n, :], left[:, 0, :]))
                settle()
                const(V.tensor_copy(left[:, 1, :], bias_split[32:33, n, :]))
                settle()
                const(V.tensor_tensor(left[:, 1, :], left[:, 0, :], left[:, 1, :], ALU.subtract))
                settle()
                const(V.tensor_copy(bias_split[64:65, n, :], left[:, 1, :]))
            settle()
            V.memset(tile_at[:, 0:1], 0).then_inc(consts_ready, 1)

            def take_turns(k):
                V.scalar_tensor_tensor(out=turns[:, k, :], in0=turns_rounded[:, k, :], scalar=-MAGIC,
                                       in1=F[k][:, :], op0=ALU.add, op1=ALU.subtract).then_inc(turns_ready, 1)

            def scale(m, k):
                z = Z[k][:, :].rearrange("p (t c) -> p t c", c=C)
                V.tensor_reduce(z_max[:, k, :], z, AX.X, ALU.max, apply_absolute_value=True).then_inc(scale_step, 1)
                dve.wait_ge(scale_step, m * 3 + 1)
                V.tensor_scalar(z_max_eps[:, k, :], z_max[:, k, :], EPS_MAX, None, ALU.add).then_inc(scale_step, 1)
                dve.wait_ge(scale_step, m * 3 + 2)
                V.reciprocal(z_inv[:, k, :], z_max_eps[:, k, :]).then_inc(scale_step, 1)
                dve.wait_ge(scale_step, m * 3 + 3)
                V.tensor_tensor(z_scaled[:, k, :, :], z, z_inv[:, k, :].unsqueeze(2).broadcast_to([P, CH, C]),
                                ALU.mult).then_inc(scaled, 1)

            def weight_scale():
                dve.wait_ge(w_step, E)
                V.tensor_reduce(w_max[:, :], w_max_e[:, :], AX.X, ALU.max).then_inc(max_ready, 1)

            def weight_scale_end():
                dve.wait_ge(max_all, 1)
                V.tensor_scalar(w_power[:, :].bitcast(I32), w_max_all[:, :].bitcast(I32), 0x7F800000, None,
                                ALU.bitwise_and).then_inc(w_step, 1)
                dve.wait_ge(w_step, E + 1)
                V.tensor_scalar(w_power[:, :], w_power[:, :], 2.0 ** -100, None, ALU.max).then_inc(w_step, 1)
                dve.wait_ge(w_step, E + 2)
                V.reciprocal(w_inv[:, :], w_power[:, :]).then_inc(w_step, 1)
                V.tensor_scalar(unscale[:, :], w_power[:, :], 1.0 / (W_TOP * X_SCALE), None, ALU.mult)\
                    .then_inc(w_step, 1)
                dve.wait_ge(w_step, E + 4)
                V.tensor_scalar(w_scale[:, :], w_inv[:, :], W_TOP, None, ALU.mult).then_inc(scale_ready, 1)

            step = [0]

            def link(ins):
                step[0] += 1
                ins.then_inc(route_step, 1)
                dve.wait_ge(route_step, step[0])

            def over_e(x):
                return x.unsqueeze(2).broadcast_to([P, NTG, E])

            def gate_q(b):
                dve.wait_ge(q_ready, NSEQ + (b // SG + 1) * ITEMS - SG + b % SG + 1)
                dve.wait_ge(v_done, b + 1)
                if b >= 2:
                    dve.wait_ge(proj_done, b - 1)
                V.scalar_tensor_tensor(out=gated[:, b % 2, :], in0=bank[6][:, :], scalar=b_v[:, 0:1],
                                       in1=q[:, b, PAD:PAD + LEN], op0=ALU.add, op1=ALU.mult).then_inc(gated_ready, 1)

            def add_x(b):
                if b == 0:
                    dve.wait_ge(loaded_rows, 16)
                dve.wait_ge(proj_done, b + 1)
                rows = x1[:, b * CH:(b + 1) * CH, :].rearrange("p t c -> p (t c)")
                V.tensor_tensor(rows, bank[7][:, :], rows, ALU.add).then_inc(res_ready, 1)
                dve.wait_ge(res_ready, b + 1)
                for j in range(b * CH, (b + 1) * CH):
                    V.bn_stats(stats[:, j, :], x1[:, j, :]).then_inc(stats_step, 1)
                for j in range(b * CH, (b + 1) * CH):
                    dve.wait_ge(stats_step, j + 1)
                    V.bn_aggr(mean_var[:, j, :], stats[:, j, :]).then_inc(norm_step, 1)

            def choose(k, values):
                link(V.tensor_tensor(work[:, :, :], values, over_e(col[:, :]), ALU.is_equal))
                link(V.tensor_tensor(work[:, :, :], work[:, :, :], rank_key[:, :, :], ALU.mult))
                link(V.tensor_reduce(col[:, :], work[:, :, :], AX.X, ALU.max))
                link(V.tensor_tensor(pick[k][:, :, :], rank_key[:, :, :], over_e(col[:, :]), ALU.is_equal))

            def norm_and_route(g, n):
                t0, t1 = g * NTG, (g + 1) * NTG
                if n < 2 * SG:
                    (gate_q, add_x)[n % 2](g * SG + n // 2)
                if n == 2 * SG:
                    dve.wait_ge(std_ready, g + 1)
                    V.reciprocal(rstd[:, t0:t1], std[:, t0:t1]).then_inc(norm_step, 1)
                    dve.wait_ge(norm_step, t1 + g + 1)
                if 2 * SG <= n < 3 * SG:
                    b = g * SG + n - 2 * SG
                    for j in range(b * CH, (b + 1) * CH):
                        V.tensor_scalar(x1[:, j, :], x1[:, j, :], mean_var[:, j, 0:1], rstd[:, j:j + 1],
                                        ALU.subtract, ALU.mult).then_inc(x1_ready, 1)
                if n == 13:
                    dve.wait_ge(high_sent, TOPK * g + 1)
                    dve.wait_ge(x1_ready, t1)
                    V.scalar_tensor_tensor(out=send[:, :, 0, C // 2:C].bitcast(F16), in0=x1[:, t0:t1, :],
                                           scalar=X_SCALE, in1=send[:, :, 0, 0:C // 2].bitcast(F16), op0=ALU.mult,
                                           op1=ALU.subtract).then_inc(moved, 1)
                if n == 14:
                    dve.wait_ge(gate_read, (g + 1) * SG)
                    dve.wait_ge(iota_done, 3)
                    link(V.tensor_copy(logits[:, :, :], bank[7][:, 0:NTG * E].rearrange("p (t e) -> p t e", e=E)))
                    link(V.tensor_reduce(col[:, :], logits[:, :, :], AX.X, ALU.max))
                    V.tensor_tensor(shifted[:, :, :], logits[:, :, :], over_e(col[:, :]), ALU.subtract)\
                        .then_inc(shifted_ready, 1)
                    dve.wait_ge(shifted_ready, g + 1)
                    choose(0, logits[:, :, :])
                if n == 15:
                    link(V.scalar_tensor_tensor(out=masked[:, :, :], in0=pick[0][:, :, :], scalar=NEG,
                                                in1=logits[:, :, :], op0=ALU.mult, op1=ALU.add))
                    link(V.tensor_reduce(col[:, :], masked[:, :, :], AX.X, ALU.max))
                    choose(1, masked[:, :, :])
                    V.tensor_tensor(picked[:, :, :], pick[0][:, :, :], pick[1][:, :, :], ALU.add)\
                        .then_inc(picked_ready, 1)
                if n == 16:
                    dve.wait_ge(exp_done, g + 1)
                    link(V.tensor_reduce(col[:, :], probs[:, :, :], AX.X, ALU.add))
                    link(V.reciprocal(wsum[:, :], col[:, :]))
                    link(V.tensor_tensor(probs[:, :, :], probs[:, :, :], over_e(wsum[:, :]), ALU.mult))
                    for k in range(TOPK):
                        link(V.tensor_tensor(work[:, :, :], probs[:, :, :], pick[k][:, :, :], ALU.mult))
                        link(V.tensor_reduce(weight_raw[:, k, :], work[:, :, :], AX.X, ALU.add))
                if n == 17:
                    link(V.tensor_tensor(col[:, :], weight_raw[:, 0, :], weight_raw[:, 1, :], ALU.add))
                    link(V.reciprocal(wsum[:, :], col[:, :]))
                    dve.wait_ge(high_sent, TOPK * g + 1)
                    for k in range(TOPK):
                        link(V.tensor_tensor(send[:, :, k, C], weight_raw[:, k, :], wsum[:, :], ALU.mult))
                    dve.wait_ge(target_ready, 1)
                    V.tensor_copy(send[:, :, :, C + 1].bitcast(U32), target[:, t0:t1, :]).then_inc(moved, 1)
                    dve.wait_ge(counts_done, 2 * (g + 1))
                    link(V.tensor_copy(tile_count[:, :, :],
                                       bank[6][:, NTG * E:2 * NTG * E].rearrange("p (t e) -> p t e", e=E)))
                if n == 18:
                    for e in range(E):
                        V.tensor_tensor_scan(out=count_to[:, :, e], data0=ones_f[:, 0:NTG], data1=tile_count[:, :, e],
                                             initial=0.0, op0=ALU.mult, op1=ALU.add).then_inc(scan_step, 1)
                    dve.wait_ge(scan_step, E * (g + 1))
                    link(V.tensor_scalar(e_tiles[:, :], count_to[:, NTG - 1, :], 1.0 / P, (P / 2 - 0.5) / P, ALU.mult,
                                         ALU.add))
                    link(V.tensor_scalar(e_tiles_r[:, :], e_tiles[:, :], MAGIC, None, ALU.add))
                    link(V.tensor_scalar(e_tiles[:, :], e_tiles_r[:, :], -MAGIC, None, ALU.add))
                    link(V.tensor_tensor_scan(out=e_end[:, :], data0=ones_f[:, 0:E], data1=e_tiles[:, :], initial=0.0,
                                              op0=ALU.mult, op1=ALU.add))
                if n == 19:
                    link(V.tensor_tensor(e_base[:, :], e_end[:, :], e_tiles[:, :], ALU.subtract))
                    link(V.tensor_tensor(place[:, :, :], count_to[:, :, :], tile_count[:, :, :], ALU.subtract))
                    link(V.tensor_tensor(place[:, :, :], bank[6][:, 0:NTG * E].rearrange("p (t e) -> p t e", e=E),
                                         place[:, :, :], ALU.add))
                    link(V.tensor_scalar(e_base[:, :], e_base[:, :], float(P), float(g * TG * P), ALU.mult, ALU.add))
                    link(V.tensor_tensor(place[:, :, :], place[:, :, :],
                                         e_base[:, :].unsqueeze(1).broadcast_to([P, NTG, E]), ALU.add))
                    for k in range(TOPK):
                        link(V.tensor_tensor(work[:, :, :], place[:, :, :], pick[k][:, :, :], ALU.mult))
                        link(V.tensor_reduce(pos_f[:, k, t0:t1], work[:, :, :], AX.X, ALU.add))
                    dve.wait_ge(rows_step, g + 1)
                    dve.wait_ge(moved, 2 * (g + 1))
                    dve.wait_ge(high_sent, TOPK * (g + 1))
                    V.tensor_copy(pos[:, :, t0:t1], pos_f[:, :, t0:t1]).then_inc(rows_ready, 1)
                if n == PARTS - 1:
                    link(V.tensor_tensor(tile_ge[:, :, :], tile_no[:, :, :],
                                         e_end[0:1, :].unsqueeze(1).broadcast_to([1, TG, E]), ALU.is_ge))
                    link(V.tensor_reduce(tile_expert_f[:, :], tile_ge[:, :, :], AX.X, ALU.add))
                    V.tensor_scalar(tile_at[:, 1 + g * TG:1 + (g + 1) * TG], tile_expert_f[:, :], float(E - 1),
                                    float(HC * C), ALU.min, ALU.mult).then_inc(routed, 1)
                    dve.wait_ge(routed, g + 1)

            def scan(g):
                first = g * ITEMS
                for b in range(SG):
                    m = first + b
                    dve.wait_ge(rounded, m + 1)
                    if m >= 2:
                        dve.wait_ge(waves_ready, m - 1)
                    take_turns(b % 2)
                    if b >= 1:
                        dve.wait_ge(z_done, m)
                        if m >= 3:
                            dve.wait_ge(turned, m - 2)
                        scale(m - 1, (b - 1) % 2)

                def item(s, b):
                    m = s * SG + (first + b)
                    dve.wait_ge(rounded, m + 1)
                    dve.wait_ge(waves_ready, m - 1)
                    take_turns(b % 2)
                    dve.wait_ge(z_done, m)
                    dve.wait_ge(turned, m - 2)
                    scale(m - 1, (b - 1) % 2)

                if g == 0:
                    dve.wait_ge(loaded_experts, 32)
                    with dve.Fori(1, STEPS) as s:
                        for b in range(SG):
                            item(s, b)
                            if b == 0:
                                V.tensor_reduce(w_max_e[:, bass.ds(s - 1, 1)],
                                                w_raw[:, bass.ds(s - 1, 1), :].rearrange("p a n -> p (a n)"), AX.X,
                                                ALU.max, apply_absolute_value=True).then_inc(w_step, 1)
                else:
                    for s in range(1, 1 + PART_STEPS):
                        for b in range(SG):
                            item(s, b)
                            norm_and_route(g - 1, (s - 1) * SG + b)
                    with dve.Fori(1 + PART_STEPS, STEPS) as s:
                        for b in range(SG):
                            item(s, b)
                end = first + ITEMS
                dve.wait_ge(z_done, end)
                dve.wait_ge(turned, end - 2)
                scale(end - 1, (SG - 1) % 2)

            for g in range(GROUPS):
                scan(g)
                if g == 0:
                    weight_scale()
                    weight_scale_end()

            def take_cols(i, k, r, again):
                dve.wait_ge(row_turned, i + 1)
                if not isinstance(i, int) or i >= 2:
                    dve.wait_ge(up_done, i - 1)
                V.tensor_copy(col_tile[:, k, :, :].rearrange("p a n -> p (a n)"),
                              bank[4][:, 0:P].bitcast(F16)).then_inc(col_ready, 1)
                if not isinstance(again, int) or again >= 1:
                    dve.wait_ge(y_stored[r], again * 16)
                V.tensor_copy(meta[:, r, :].bitcast(U32), row_tile[:, k, C:ROW].bitcast(U32)).then_inc(meta_ready, 1)

            def slot(quad, r, last=False):
                i = quad * 4 + r
                k = r % 2
                if not last:
                    take_cols(i + 1, 1 - k, (r + 1) % 4, quad if r < 3 else quad + 1)
                dve.wait_ge(act_ready, i + 1)
                dve.wait_ge(up_done, i + 1)
                if not isinstance(i, int) or i >= 2:
                    dve.wait_ge(y_done, i - 1)
                V.scalar_tensor_tensor(out=hidden[:, k, :], in0=bank[2 + k][:, :], scalar=unscale[:, 0:1],
                                       in1=act_gate[:, k, :], op0=ALU.mult, op1=ALU.mult).then_inc(hidden_ready, 1)
                if isinstance(i, int) and i < PARTS:
                    norm_and_route(1, i)

            def add_up(pair, k, fetched):
                dve.wait_ge(y_fetched[k], fetched * 16)
                V.tensor_tensor(y_sum[:, k, :, :], y_back[:, k, :, 0, :], y_back[:, k, :, 1, :], ALU.add)\
                    .then_inc(y_summed, 1)
                dve.wait_ge(y_summed, pair + 1)
                V.tensor_tensor(x1[:, bass.ds(pair * 2, 2), :], x1[:, bass.ds(pair * 2, 2), :], y_sum[:, k, :, :],
                                ALU.add).then_inc(merged, 1)
                dve.wait_ge(merged, pair + 1)
                for n in range(2):
                    V.bn_stats(stats2[:, bass.ds(pair * 2 + n, 1), :].rearrange("p a n -> p (a n)"),
                               x1[:, bass.ds(pair * 2 + n, 1), :].rearrange("p a n -> p (a n)"))\
                        .then_inc(stats2_ready, 1)

            take_cols(0, 0, 0, 0)
            for quad in range(PART_QUADS):
                for r in range(4):
                    slot(quad, r)
            with dve.Fori(PART_QUADS, TG // 4 + 2) as quad:
                for r in range(4):
                    slot(quad, r)
            with dve.Fori(0, NTG // 4 - 1) as n:
                for k in range(2):
                    quad = n * 2 + (k + TG // 4 + 2)
                    for r in range(4):
                        slot(quad, r)
                    add_up(n * 2 + k, k, n + 1)
            quad = QUADS - 2
            for r in range(4):
                slot(quad, r)
            add_up(NTG // 2 - 2, 0, NTG // 4)
            for r in range(4):
                slot(QUADS - 1, r, last=(r == 3))
            add_up(NTG // 2 - 1, 1, NTG // 4)
            for pair in range(NTG // 2, NT // 2):
                add_up(pair, pair % 2, pair // 2 + 1)
            for j in range(NT):
                dve.wait_ge(stats2_ready, j + 1)
                V.bn_aggr(mean_var2[:, j, :], stats2[:, j, :]).then_inc(var_ready, 1)
            dve.wait_ge(std2_ready, 1)
            V.reciprocal(rstd2[:, :], std2[:, :]).then_inc(rstd2_ready, 1)
            dve.wait_ge(rstd2_ready, 1)
            for j in range(NT):
                V.tensor_scalar(x1[:, j, :], x1[:, j, :], mean_var2[:, j, 0:1], rstd2[:, j:j + 1],
                                ALU.subtract, ALU.mult).then_inc(out_ready, 1)


def kernel(**inputs):
    import numpy as np
    import concourse.bacc as bacc
    from concourse.bass_utils import run_bass_kernel_spmd

    a = {k: np.asarray(v) for k, v in inputs.items()}
    x = a["L0_attn_x"].reshape(NT * P, C)
    fw = a["L0_attn_freq_W"].reshape(2, C, P // 2)
    fb = a["L0_attn_freq_b"]
    host = {
        "x_rows": x.reshape(NT, P, C).transpose(1, 0, 2),
        "x_cols": x.T,
        "attn_W": a["L0_attn_attn_W"],
        "attn_bq": a["L0_attn_attn_b"][:C].reshape(C, 1),
        "attn_bv": a["L0_attn_attn_b"][C:].reshape(C, 1),
        "freq_W": np.concatenate([fw, fw], axis=2).transpose(1, 0, 2),
        "freq_b": np.concatenate([fb, fb]).reshape(1, P),
        "out_W": a["L0_attn_out_W"],
        "out_b": a["L0_attn_out_b"].reshape(1, C),
        "proj_W": a["L0_attn_proj_W"],
        "proj_b": a["L0_attn_proj_b"].reshape(1, C),
        "ident_col": a["L0_attn_identity"].reshape(C, 1),
        "gate_T": a["L0_ffn_gate_w"].T,
        "gu_T": a["L0_ffn_gate_up_proj"].transpose(2, 0, 1),
        "dn_T": a["L0_ffn_down_proj"].transpose(0, 2, 1).reshape(E, HC, P, C).transpose(2, 0, 1, 3),
    }
    nc = bacc.Bacc("TRN2", target_bir_lowering=False, num_devices=1)
    arrays, args = {}, []
    for name, v in host.items():
        v = np.ascontiguousarray(v)
        arrays[name] = v
        args.append(nc.dram_tensor(name, v.shape, mybir.dt.from_np(v.dtype), kind="ExternalInput").ap())
    out = nc.dram_tensor("out_rows", (NT * P, C), F32, kind="ExternalOutput").ap()
    build(nc, *args, out)
    r = run_bass_kernel_spmd(nc, [arrays], core_ids=[0])
    return r.results[0]["out_rows"].reshape(NSEQ, LEN, C)
```

```python
from contextlib import ExitStack

import concourse.bass as bass
from concourse import mybir

ALU = mybir.AluOpType
ACT = mybir.ActivationFunctionType
AX = mybir.AxisListType
F32 = mybir.dt.float32
F32R = mybir.dt.float32r
F16 = mybir.dt.float16
BF16 = mybir.dt.bfloat16
I32 = mybir.dt.int32
U32 = mybir.dt.uint32

P = 128
NSEQ, LEN, C = 8, 512, 128
STEPS = 9
PAD = LEN // 2
CH = LEN // P
NT = NSEQ * CH
GROUPS = 2
SG, NTG = NSEQ // GROUPS, NT // GROUPS
E, HID = 8, 512
HC = HID // P
TOPK = 2
TG = NTG * TOPK + E
TILES = GROUPS * TG
ROW = C + 2
ITEMS = STEPS * SG
QUADS = TILES // 4
PARTS = 21
PART_STEPS = 6
PART_FROM = 1
EARLY_PARTS = 1
PART_QUADS = 6
RUN = 8
PART_RUNS = PART_QUADS * 4 // RUN
MAX_FROM = 2
MAX_STEPS = E // 2
SPLIT_FROM = (MAX_FROM + MAX_STEPS) * SG + 3
SEND_FROM = PART_FROM + PARTS - 3
LOW_BY_DVE = SEND_FROM + 2
XT_PARTS = 4
X_SCALE = 2.0 ** 10
W_TOP = 2.0 ** 14
EPS_MAX, EPS_LN = 1e-6, 1e-5
MAGIC = 1.5 * 2.0 ** 23
INV_TWO_PI = 0.15915494309189535
TWO_PI = 6.2831850
NEG = -3.0e38


def build(nc, x_rows, x_cols, attn_params, weights, biases, gu_T, dn_T, out):
    ctx = ExitStack()
    with ctx:
        def sb(name, shape, dt=F32):
            return ctx.enter_context(nc.sbuf_tensor(name, shape, dt))

        def ps(name, shape, dt=F32):
            return ctx.enter_context(nc.psum_tensor(name, shape, dt))

        def sem(name):
            return ctx.enter_context(nc.semaphore(name))

        attn_pack = sb("attn_pack", [P, 2 * C + 3])
        w_attn, b_q, b_v = attn_pack[:, 0:2 * C], attn_pack[:, 2 * C:2 * C + 1], attn_pack[:, 2 * C + 1:2 * C + 2]
        idc = attn_pack[:, 2 * C + 2:2 * C + 3]
        w_pack = sb("w_pack", [P, 4 * C + E])
        w_freq_raw = w_pack[:, 0:2 * C].rearrange("p (a n) -> p a n", a=2)
        w_out, w_proj, w_gate = w_pack[:, 2 * C:3 * C], w_pack[:, 3 * C:4 * C], w_pack[:, 4 * C:4 * C + E]
        w_freq_high = sb("w_freq_high", [P, 2, P], F32R)
        w_freq_low = sb("w_freq_low", [P, 2, P], F32R)
        w_raw = sb("w_raw", [P, E, 2 * HID])
        w_high = sb("w_high", [P, E, 2 * HID], F16)
        w_low = sb("w_low", [P, E, 2 * HID], F16)
        w_max_e = sb("w_max_e", [P, E])
        w_max = sb("w_max", [P, 1])
        w_max_all = sb("w_max_all", [P, 1])
        w_power = sb("w_power", [P, 1])
        w_inv = sb("w_inv", [P, 1])
        w_scale = sb("w_scale", [P, 1])
        unscale = sb("unscale", [P, 1])
        w_dn = sb("w_dn", [P, E, HC, C])
        bias_row = sb("bias_row", [1, 3, P])
        bias_split = sb("bias_split", [P, 3, P], BF16)
        ones_bf = sb("ones_bf", [P, LEN], BF16)
        iota_p = sb("iota_p", [P, P])
        identity = sb("identity", [P, P])
        identity_h = sb("identity_h", [P, P], F16)
        before = sb("before", [P, P], BF16)
        xT = sb("xT", [P, NT, P])
        x1 = sb("x1", [P, NT, C])
        q_high = sb("q_high", [P, NSEQ, PAD + LEN], F32R)
        q_low = sb("q_low", [P, SG, PAD + LEN], F32R)
        turns = sb("turns", [P, 2, LEN])
        waves = sb("waves", [P, 2, LEN])
        z_scaled = sb("z_scaled", [P, 2, CH, C])
        z_max = sb("z_max", [P, 2, CH])
        z_max_eps = sb("z_max_eps", [P, 2, CH])
        z_inv = sb("z_inv", [P, 2, CH])
        x1T = sb("x1T", [P, 2, LEN])
        gated = x1T
        bias_left = x1T[0:1, :, 0:3 * P].rearrange("p k (n c) -> p k n c", n=3)
        stats = sb("stats", [P, NT, 6])
        mean_var = sb("mean_var", [P, NT, 2])
        std = sb("std", [P, NT])
        rstd = sb("rstd", [P, NT])
        shifted = sb("shifted", [P, NTG, E])
        probs = sb("probs", [P, NTG, E])
        rank_key = sb("rank_key", [P, NTG, E])
        work = sb("work", [P, NTG, E])
        pick = [sb(f"pick{k}", [P, NTG, E]) for k in range(TOPK)]
        masked = sb("masked", [P, NTG, E])
        picked = sb("picked", [P, NTG, E], BF16)
        col = sb("col", [P, NTG])
        weight_raw = sb("weight_raw", [P, TOPK, NTG])
        wsum = sb("wsum", [P, NTG])
        ones_f = sb("ones_f", [P, NT])
        count_to = sb("count_to", [P, NTG, E])
        place = sb("place", [P, NTG, E])
        e_tiles = sb("e_tiles", [P, E])
        e_tiles_r = sb("e_tiles_r", [P, E])
        e_end = sb("e_end", [P, E])
        e_base = sb("e_base", [P, E])
        pos_f = sb("pos_f", [P, TOPK, NT])
        pos = sb("pos", [P, TOPK, NT], U32)
        tile_no = sb("tile_no", [1, TG, E])
        tile_ge = sb("tile_ge", [1, TG, E])
        tile_expert_f = sb("tile_expert_f", [1, TG])
        tile_at = sb("tile_at", [1, 1 + TILES], I32)
        send = sb("send", [P, NTG, TOPK, ROW])
        q_last = (send[:, :, :, :].rearrange("p t k c -> p (t k c)")[:, 0:SG * LEN], xT[:, 0:NTG, :].rearrange(
            "p t c -> p (t c)"))
        target = sb("target", [P, NT, TOPK], U32)
        rows_and_cols = sb("rows_and_cols", [P, 2 * ROW + 2 * P])
        row_tile = rows_and_cols[:, 0:2 * ROW].rearrange("p (k n) -> p k n", k=2)
        meta = sb("meta", [P, 4, 2])
        col_tile = rows_and_cols[:, 2 * ROW:2 * ROW + 2 * P].bitcast(F16).rearrange("p (k a n) -> p k a n", k=2, a=2)
        q_whole = rows_and_cols[:, 0:LEN]
        act_gate = turns
        hidden = turns
        y_tile = [z_scaled[:, r // 2, 2 + r % 2, :] for r in range(4)]
        y_back = waves[:, :, :].rearrange("p n (t k c) -> p n t k c", t=2, k=TOPK)
        y_sum = z_scaled[:, :, 0:2, :]
        y_last = w_raw[:, 0:4, :].rearrange("p n (t k c) -> p n t k c", t=CH, k=TOPK)
        stats2 = sb("stats2", [P, NT, 6])
        mean_var2 = sb("mean_var2", [P, NT, 2])
        std2 = sb("std2", [P, NT])
        rstd2 = sb("rstd2", [P, NT])
        shift2 = sb("shift2", [P, NT])
        eps_ln = sb("eps_ln", [P, 1])
        table_scratch = sb("table_scratch", [P, 1])

        def first_whole(b):
            return (waves if b < SG else gated)[:, b % 2, :]

        bank = [ps(f"bank{i}", [P, LEN]) for i in range(8)]
        F, Z, T = bank[0:2], bank[2:4], bank[4:6]
        logits = bank[7][:, 0:NTG * E].rearrange("p (t e) -> p t e", e=E)
        before_in_tile, tile_count = [bank[6][:, n * NTG * E:(n + 1) * NTG * E].rearrange("p (t e) -> p t e", e=E)
                                      for n in range(2)]

        sorted_x = nc.dram_tensor("sorted_x", [TILES * P, ROW], F32, kind="Internal").ap()
        y_tok = nc.dram_tensor("y_tok", [NT * P * TOPK + TILES * P, C], F32, kind="Internal").ap()

        loaded_q = sem("loaded_q")
        loaded_xT = [sem(f"loaded_xT{k}") for k in range(XT_PARTS)]
        loaded_freq = sem("loaded_freq")
        loaded_rows = sem("loaded_rows")
        loaded_experts = sem("loaded_experts")
        iota_done = sem("iota_done")
        const_step = sem("const_step")
        consts_ready = sem("consts_ready")
        blank_ready = sem("blank_ready")
        filled = sem("filled")
        max_ready = sem("max_ready")
        max_all = sem("max_all")
        scale_ready = sem("scale_ready")
        w_step = sem("w_step")
        high_ready = sem("high_ready")
        low_ready = sem("low_ready")
        high_sent = sem("high_sent")
        low_sent = sem("low_sent")
        q0_done = sem("q0_done")
        q0_ready = sem("q0_ready")
        q0_low_ready = sem("q0_low_ready")
        q_low_ready = sem("q_low_ready")
        q_taken = sem("q_taken")
        loaded_gate_up = sem("loaded_gate_up")
        v_done = sem("v_done")
        q_ready = sem("q_ready")
        f_done = sem("f_done")
        rounded = sem("rounded")
        turns_ready = sem("turns_ready")
        waves_ready = sem("waves_ready")
        z_done = sem("z_done")
        scale_step = sem("scale_step")
        scaled = sem("scaled")
        turned = sem("turned")
        gated_ready = sem("gated_ready")
        proj_done = sem("proj_done")
        res_ready = sem("res_ready")
        norm_step = sem("norm_step")
        std_ready = sem("std_ready")
        x1_ready = sem("x1_ready")
        x1T_done = sem("x1T_done")
        x1T_ready = sem("x1T_ready")
        route_step = sem("route_step")
        exp_done = sem("exp_done")
        counts_done = sem("counts_done")
        picked_ready = sem("picked_ready")
        shifted_ready = sem("shifted_ready")
        routed = sem("routed")
        sent = sem("sent")
        row_loaded = [sem(f"row_loaded{k}") for k in range(2)]
        row_turned = sem("row_turned")
        col_ready = sem("col_ready")
        gate_done = sem("gate_done")
        up_done = sem("up_done")
        act_ready = sem("act_ready")
        hidden_ready = sem("hidden_ready")
        meta_ready = sem("meta_ready")
        y_done = sem("y_done")
        y_ready = sem("y_ready")
        y_stored = [sem(f"y_stored{k}") for k in range(4)]
        y_fetched = [sem(f"y_fetched{k}") for k in range(2)]
        y_summed = sem("y_summed")
        merged = sem("merged")
        stats2_ready = sem("stats2_ready")
        var_ready = sem("var_ready")
        std2_ready = sem("std2_ready")
        rstd2_ready = sem("rstd2_ready")
        out_ready = sem("out_ready")
        out_ready_last = sem("out_ready_last")
        y_last_fetched = [sem(f"y_last_fetched{n}") for n in range(SG)]
        y_last_summed = sem("y_last_summed")
        shift_ready = sem("shift_ready")
        out_stored = sem("out_stored")
        send_step = sem("send_step")
        rows_ready = sem("rows_ready")
        moved = sem("moved")
        y_taken = sem("y_taken")
        target_ready = sem("target_ready")
        rows_step = sem("rows_step")
        scan_step = sem("scan_step")
        stats_step = sem("stats_step")
        gate_read = sem("gate_read")

        block = ctx.enter_context(nc.Block())
        @block.sync
        def _(sp):
            def load_xT(n):
                wide = NT // XT_PARTS
                sp.dma_start(xT[:, n * wide:(n + 1) * wide, :],
                             x_cols[:, n * wide * P:(n + 1) * wide * P].rearrange("c (t p) -> c t p", p=P))\
                    .then_inc(loaded_xT[n], 16)

            sp.dma_start(attn_pack[:, :], attn_params).then_inc(loaded_q, 16)
            load_xT(0)
            sp.dma_start(bias_row[:, :, :], biases).then_inc(loaded_freq, 16)
            sp.dma_start(w_pack[:, :], weights).then_inc(loaded_freq, 16)
            for n in range(1, XT_PARTS):
                load_xT(n)
            sp.dma_start(x1[:, :, :], x_rows).then_inc(loaded_rows, 16)
            sp.dma_start(w_raw[:, :, :], gu_T).then_inc(loaded_gate_up, 16)
            sp.dma_start(w_dn[:, :, :, :], dn_T).then_inc(loaded_experts, 16)

            def load_rows(i, k):
                if not isinstance(i, int) or i >= 2:
                    sp.wait_ge(row_turned, i - 1)
                    sp.wait_ge(meta_ready, i - 1)
                sp.dma_start(row_tile[:, k, :], sorted_x[bass.ds(i * P, P), :]).then_inc(row_loaded[k], 16)

            def load_y(pair, k, half):
                if half:
                    sp.wait_ge(y_summed, pair - 1)
                sp.dma_start(y_back[:, k, :, :, :],
                             y_tok[bass.ds(pair * 2 * P * TOPK, 2 * P * TOPK), :].rearrange(
                                 "(t p k) c -> p t k c", p=P, k=TOPK)).then_inc(y_fetched[k], 16)

            sp.wait_ge(sent, 16 * TOPK * NTG)
            sp.wait_ge(q_low_ready, GROUPS * (ITEMS - SG))
            for i in range(4):
                load_rows(i, i % 2)
            with sp.Fori(1, TG // 4) as quad:
                for r in range(4):
                    load_rows(quad * 4 + r, r % 2)
            sp.wait_ge(sent, 16 * TOPK * NT)
            with sp.Fori(TG // 4, TG // 4 + 2) as quad:
                for r in range(4):
                    load_rows(quad * 4 + r, r % 2)
            for r in range(4):
                sp.wait_ge(y_stored[r], 16 * (TG // 4))
            load_y(0, 0, False)
            load_y(1, 1, False)
            for r in range(4):
                load_rows((TG // 4 + 2) * 4 + r, r % 2)
            for r in range(4):
                load_rows((TG // 4 + 3) * 4 + r, r % 2)
            with sp.Fori(1, NTG // 4) as n:
                for k in range(2):
                    load_y(n * 2 + k, k, True)
                    for r in range(4):
                        load_rows((n * 2 + (k + TG // 4 + 2)) * 4 + r, r % 2)
            sp.wait_ge(high_ready, 2 * E)
            sp.wait_ge(low_ready, 2 * E)
            for r in range(4):
                sp.wait_ge(y_stored[r], 16 * QUADS)
            for b in range(SG, NSEQ):
                sp.dma_start(y_last[:, b - SG, :, :, :],
                             y_tok[b * LEN * TOPK:(b + 1) * LEN * TOPK, :].rearrange("(t p k) c -> p t k c", p=P, k=TOPK))\
                    .then_inc(y_last_fetched[b - SG], 16)
            for b in range(NSEQ):
                sp.wait_ge(out_ready if b < SG else out_ready_last, (b % SG + 1) * CH)
                sp.dma_start(out[b * LEN:(b + 1) * LEN, :].rearrange("(t p) c -> p t c", p=P),
                             x1[:, b * CH:(b + 1) * CH, :]).then_inc(out_stored, 16)
            sp.wait_ge(out_stored, 16 * NSEQ)

        @block.gpsimd
        def _(pool):
            nc.gpsimd.iota(iota_p[:, :], pattern=[[1, P]], base=0, channel_multiplier=-1,
                           allow_small_or_imprecise_dtypes=True).then_inc(iota_done, 1)
            nc.gpsimd.iota(tile_no[:, :, :], pattern=[[1, TG], [0, E]], base=0, channel_multiplier=0,
                           allow_small_or_imprecise_dtypes=True).then_inc(iota_done, 1)
            nc.gpsimd.iota(rank_key[:, :, :], pattern=[[0, NTG], [-1, E]], base=E, channel_multiplier=0,
                           allow_small_or_imprecise_dtypes=True).then_inc(iota_done, 1)
            nc.gpsimd.iota(target[:, :, :], pattern=[[P * TOPK, NT], [1, TOPK]], base=0,
                           channel_multiplier=TOPK).then_inc(target_ready, 1)
            slots = send[:, :, :, :].rearrange("p t k c -> p (t k) c")

            def fill(n):
                at = n * NTG * TOPK
                wide = min(NTG * TOPK, TILES - at)
                if n:
                    pool.wait_ge(filled, 16 * n)
                nc.gpsimd.iota(slots[:, 0:wide, C + 1:C + 2].bitcast(U32), pattern=[[P, wide], [0, 1]],
                               base=NT * P * TOPK + at * P, channel_multiplier=1).then_inc(send_step, 1)
                pool.wait_ge(send_step, n + 1)
                pool.dma_start(sorted_x[at * P:(at + wide) * P, :].rearrange("(t p) c -> p t c", p=P),
                               slots[:, 0:wide, :]).then_inc(filled, 16)

            def low_part(b, whole):
                return nc.gpsimd.tensor_tensor(q_low[:, b % SG, PAD:PAD + LEN], whole,
                                               q_high[:, b, PAD:PAD + LEN].bitcast(F32), ALU.subtract)

            def first_low(b):
                pool.wait_ge(q0_ready, b + 1)
                low_part(b, first_whole(b)).then_inc(q0_low_ready, 1)

            def item(m, b):
                pool.wait_ge(q_ready, m + 1)
                if not isinstance(m, int):
                    pool.sem_inc(q_taken, 1)
                low_part(b, q_whole).then_inc(q_low_ready, 1)

            def send_rows(j, k):
                nc.gpsimd.indirect_dma_start(
                    out=sorted_x, out_offset=bass.IndirectOffsetOnAxis(ap=pos[:, k, j:j + 1], axis=0),
                    in_=send[:, j % NTG, k, :], in_offset=None).then_inc(sent, 16)

            def store_y(r):
                nc.gpsimd.indirect_dma_start(
                    out=y_tok, out_offset=bass.IndirectOffsetOnAxis(ap=meta[:, r, 1:2].bitcast(U32), axis=0),
                    in_=y_tile[r], in_offset=None).then_inc(y_stored[r], 16)

            def weight_low(n):
                if not 0 <= n < 2 * E:
                    return
                e, part = n // 2, slice(n % 2 * HID, (n % 2 + 1) * HID)
                pool.wait_ge(high_ready, 2 * (e + 1))
                nc.gpsimd.tensor_tensor(w_low[:, e, part], w_raw[:, e, part], w_high[:, e, part], ALU.subtract)\
                    .then_inc(low_ready, 1)

            for b in range(SG):
                first_low(b)
            for b in range(SG):
                item(b, b)
            pool.wait_ge(blank_ready, SG)
            fill(0)
            with pool.Fori(1, 3) as step:
                for b in range(SG):
                    item(step * SG + b, b)
            fill(1)
            scale_step_no = MAX_FROM + MAX_STEPS - 1
            with pool.Fori(3, scale_step_no) as step:
                for b in range(SG):
                    item(step * SG + b, b)
            fill(2)
            for step in range(scale_step_no, STEPS):
                for b in range(SG):
                    if step < STEPS - 1:
                        item(step * SG + b, b)
                    elif b >= 1:
                        first_low(SG + b - 1)
                    weight_low(step * SG + b - SPLIT_FROM)
                    if step * SG + b == SPLIT_FROM - 6:
                        pool.wait_ge(max_ready, 1)
                        nc.gpsimd.partition_all_reduce(w_max_all[:, :], w_max[:, :], P, bass.bass_isa.ReduceOp.max)\
                            .then_inc(max_all, 1)
            pool.wait_ge(filled, 16 * 3)
            first_low(NSEQ - 1)
            for n in range(ITEMS - SG):
                if n < LOW_BY_DVE:
                    item(ITEMS + n, SG + n % SG)
                weight_low(ITEMS + n - SPLIT_FROM)
                if n >= SEND_FROM:
                    pool.wait_ge(rows_ready, 1)
                    for k in range(TOPK):
                        send_rows(n - SEND_FROM, k)
            for j in range(ITEMS - SG - SEND_FROM, NTG):
                for k in range(TOPK):
                    send_rows(j, k)
            for i in range(TG):
                n = i - PARTS + EARLY_PARTS + 2
                if n == 0:
                    pool.wait_ge(rows_ready, 2)
                if 0 <= n < NTG:
                    for k in range(TOPK):
                        send_rows(NTG + n, k)
                pool.wait_ge(y_ready, i + 1)
                store_y(i % 4)
            with pool.Fori(TG // 4, QUADS) as quad:
                for r in range(4):
                    pool.wait_ge(y_ready, quad * 4 + (r + 1))
                    pool.sem_inc(y_taken, 1)
                    store_y(r)
            for n in range(SG):
                pool.wait_ge(y_last_fetched[n], 16)
                nc.gpsimd.tensor_tensor(y_last[:, n, :, 0, :], y_last[:, n, :, 0, :], y_last[:, n, :, 1, :], ALU.add)\
                    .then_inc(y_last_summed, 1)

        @block.tensor
        def _(pe):
            def first_q(b, to):
                if b * XT_PARTS % NSEQ == 0:
                    pe.wait_ge(loaded_xT[b * XT_PARTS // NSEQ], 16)
                if b % SG >= 2:
                    pe.wait_ge(q0_ready, b - 1)
                nc.tensor.matmul(to[:, :], w_attn[:, 0:C], xT[:, b * CH:(b + 1) * CH, :],
                                 start=True, stop=True).then_inc(q0_done, 1)

            pe.wait_ge(loaded_q, 16)
            for b in range(SG):
                first_q(b, F[b % 2])

            def angles(b, shift, low_ready, low_count):
                k = b % 2
                nc.tensor.matmul(F[k][:, :], bias_split[:, 0, :], ones_bf[:, :], start=True, stop=False)
                spans = ((0, bass.ds(PAD - shift, LEN)), (1, slice(PAD, PAD + LEN)))
                for n, span in spans:
                    for w in (w_freq_low, w_freq_high):
                        nc.tensor.matmul(F[k][:, :], w[:, n, :], q_high[:, b, span], start=False, stop=False)
                pe.wait_ge(low_ready, low_count)
                for n, span in spans:
                    last = nc.tensor.matmul(F[k][:, :], w_freq_high[:, n, :], q_low[:, b % SG, span], start=False,
                                            stop=(n == 1))
                last.then_inc(f_done, 1)

            def mix(b):
                k = b % 2
                nc.tensor.matmul(Z[k][:, :], ones_bf[:, 0:P], bias_split[:, 1:2, :].broadcast_to([P, CH, P]),
                                 start=True, stop=False, skip_group_check=True)
                for c in range(CH):
                    last = nc.tensor.matmul(Z[k][:, c * P:(c + 1) * P], waves[:, k, c * P:(c + 1) * P], w_out[:, :],
                                            start=False, stop=(c == CH - 1), skip_group_check=True)
                last.then_inc(z_done, 1)

            def turn(b):
                k = b % 2
                for c in range(CH):
                    last = nc.tensor.transpose(T[k][:, c * P:(c + 1) * P], z_scaled[:, k, c, :], identity[:, :])
                last.then_inc(turned, 1)

            def values(b):
                if b % SG:
                    pe.wait_ge(gated_ready, b)
                elif b:
                    pe.wait_ge(routed, b // SG)
                nc.tensor.matmul(bank[6][:, :], w_attn[:, C:2 * C], xT[:, b * CH:(b + 1) * CH, :],
                                 start=True, stop=True).then_inc(v_done, 1)

            def project(b):
                pe.wait_ge(gated_ready, b + 1)
                if b % SG:
                    pe.wait_ge(res_ready, b)
                nc.tensor.matmul(bank[7][:, :], ones_bf[:, 0:P], bias_split[:, 2:3, :].broadcast_to([P, CH, P]),
                                 start=True, stop=False, skip_group_check=True)
                for c in range(CH):
                    last = nc.tensor.matmul(bank[7][:, c * P:(c + 1) * P], gated[:, b % 2, c * P:(c + 1) * P],
                                            w_proj[:, :], start=False, stop=(c == CH - 1), skip_group_check=True)
                last.then_inc(proj_done, 1)

            def turn_x1(b):
                pe.wait_ge(x1_ready, (b + 1) * CH)
                if b % SG:
                    pe.wait_ge(x1T_ready, b)
                for c in range(CH):
                    last = nc.tensor.transpose(bank[6][:, c * P:(c + 1) * P], x1[:, b * CH + c, :], identity[:, :])
                last.then_inc(x1T_done, 1)

            def gate(b):
                pe.wait_ge(x1T_ready, b + 1)
                if b % SG == 0:
                    pe.wait_ge(res_ready, b + SG)
                for c in range(CH):
                    j = b % SG * CH + c
                    last = nc.tensor.matmul(bank[7][:, j * E:(j + 1) * E], x1T[:, b % 2, c * P:(c + 1) * P], w_gate[:, :],
                                            start=True, stop=True, skip_group_check=True)
                last.then_inc(gate_read, 1)

            def norm_and_route(g, n):
                if g == 0 and n < 2:
                    pe.wait_ge(q0_ready, NSEQ - 1 + n)
                if n < 2 * SG:
                    (values, project)[n % 2](g * SG + n // 2)
                if 2 * SG + 2 <= n < 3 * SG + 2:
                    gate(g * SG + n - 2 * SG - 2)
                if 2 * SG + 1 <= n < 3 * SG + 1:
                    turn_x1(g * SG + n - 2 * SG - 1)
                if n == 16:
                    pe.wait_ge(picked_ready, g + 1)
                    pe.wait_ge(x1T_ready, (g + 1) * SG)
                    nc.tensor.matmul(bank[6][:, 0:NTG * E], before[:, :], picked[:, :, :], start=True, stop=True,
                                     skip_group_check=True).then_inc(counts_done, 1)
                    nc.tensor.matmul(bank[6][:, NTG * E:2 * NTG * E], ones_bf[:, 0:P], picked[:, :, :], start=True,
                                     stop=True, skip_group_check=True).then_inc(counts_done, 1)

            def scan(g):
                first = g * ITEMS
                b0 = g * SG
                for b in range(SG):
                    m = first + b
                    pe.wait_ge(q0_ready, min(b + 3, SG) if m < SG else SG + b + 1)
                    if m >= 2:
                        pe.wait_ge(turns_ready, m - 1)
                    if m < SG:
                        pe.wait_ge(consts_ready, b + 1)
                    angles(b0 + b, 1, q0_low_ready, b0 + b + 1)
                    if m == ITEMS:
                        first_q(NSEQ - 1, bank[7])
                    if m >= 1:
                        pe.wait_ge(waves_ready, m)
                        if m >= 3:
                            pe.wait_ge(scaled, m - 2)
                        mix(b0 + b - 1)
                    if m >= 2:
                        pe.wait_ge(scaled, m - 1)
                        if m >= 4:
                            pe.wait_ge(q_ready, m - 3)
                        turn(b0 + b - 2)
                    if g and b >= PART_FROM:
                        norm_and_route(g - 1, b - PART_FROM)
                def item(s, b, then_first_q=False):
                    m = s * SG + (first + b)
                    pe.wait_ge(q_ready, m - (SG - 1))
                    pe.wait_ge(turns_ready, m - 1)
                    angles(b0 + b, 1 << s, q_low_ready, m - (SG - 1 + g * SG))
                    if then_first_q:
                        first_q(SG + b - 1, bank[7 - b % 2])
                    pe.wait_ge(waves_ready, m)
                    pe.wait_ge(scaled, m - 2)
                    mix(b0 + (b - 1) % SG)
                    pe.wait_ge(scaled, m - 1)
                    pe.wait_ge(q_ready, m - 3)
                    turn(b0 + (b - 2) % SG)

                from_step = 1
                if g:
                    for s in range(1, PART_STEPS):
                        for b in range(SG):
                            item(s, b)
                            norm_and_route(g - 1, s * SG + b - PART_FROM)
                    from_step = PART_STEPS
                with pe.Fori(from_step, STEPS if g else STEPS - 1) as s:
                    for b in range(SG):
                        item(s, b)
                if g == 0:
                    for b in range(SG):
                        item(STEPS - 1, b, then_first_q=(b >= 1))

            for g in range(GROUPS):
                scan(g)

            def turn_rows(i, k):
                pe.wait_ge(row_loaded[k], (i // 2 + 1) * 16 if isinstance(i, int) else (i - k) * 8 + 16)
                if not isinstance(i, int) or i >= 1:
                    pe.wait_ge(col_ready, i)
                halves = row_tile[:, k, 0:C].bitcast(F16)
                to = bank[6 if isinstance(i, int) and i == 0 else 4][:, 0:P].bitcast(F16)
                nc.tensor.transpose(to[:, 0:P], halves[:, 0:P], identity_h[:, :])
                nc.tensor.transpose(to[:, P:2 * P], halves[:, P:2 * P], identity_h[:, :]).then_inc(row_turned, 1)

            def gate_up(k, at, half, next_down):
                for c in range(HC):
                    to = bank[2 * half + k][:, c * P:(c + 1) * P]
                    here = bass.ds(at + (half * HID + c * P), P)
                    nc.tensor.matmul(to, highs[:, here], col_tile[:, k, 1, :], start=True, stop=False,
                                     skip_group_check=True)
                    if half and (not isinstance(next_down, int) or next_down >= 0):
                        if c == HC - 2:
                            pe.wait_ge(hidden_ready, next_down + 1)
                        if c == HC - 1 and (not isinstance(next_down, int) or next_down >= 1):
                            pe.wait_ge(y_ready, next_down)
                    nc.tensor.matmul(to, highs[:, here], col_tile[:, k, 0, :], start=False, stop=False,
                                     skip_group_check=True)
                    last = nc.tensor.matmul(to, lows[:, here], col_tile[:, k, 0, :], start=False, stop=True,
                                            skip_group_check=True)
                last.then_inc((gate_done, up_done)[half], 1)

            def down(i, k, at):
                for c in range(HC):
                    last = nc.tensor.matmul(bank[5][:, 0:C], hidden[:, k, c * P:(c + 1) * P],
                                            downs[:, bass.ds(at + c * 2 * C, 2 * C)].bitcast(F32),
                                            start=(c == 0), stop=(c == HC - 1))
                last.then_inc(y_done, 1)

            highs = w_high[:, :, :].rearrange("p e n -> p (e n)")
            lows = w_low[:, :, :].rearrange("p e n -> p (e n)")
            downs = w_dn[:, :, :, :].rearrange("p e a n -> p (e a n)").bitcast(F16)
            places = [pe.alloc_register(f"place{n}") for n in range(RUN + 1)]

            def load_places(run):
                pe.reg_load(places, tile_at[0:1, bass.ds(run * RUN, RUN + 1)])

            def run_slots(run):
                at = [pe.snap(x, min_val=0, max_val=(E - 1) * 2 * HID, out_of_modulus=2 * HID) for x in places]
                for r in range(RUN):
                    i, k = run * RUN + r, r % 2
                    if not isinstance(i, int) or i + 1 < TILES:
                        turn_rows(i + 1, 1 - k)
                    if isinstance(i, int) and i == TILES - 1:
                        pe.wait_ge(col_ready, TILES)
                    if not (isinstance(i, int) and i == 0):
                        gate_up(k, at[r + 1], 0, i - 1)
                        gate_up(k, at[r + 1], 1, i - 1)
                    if not isinstance(i, int) or i >= 1:
                        down(i - 1, 1 - k, at[r])
                    if r == RUN - 1 and not (isinstance(i, int) and i == TILES - 1):
                        load_places(run + 1)
                    if isinstance(i, int) and i < PARTS - EARLY_PARTS:
                        norm_and_route(1, i + EARLY_PARTS)
                return at[RUN]

            end = GROUPS * ITEMS
            pe.wait_ge(waves_ready, end)
            pe.wait_ge(scaled, end - 2)
            mix(NSEQ - 1)
            pe.wait_ge(routed, 1)
            turn_rows(0, 0)
            pe.wait_ge(scaled, end - 1)
            pe.wait_ge(q_ready, end - 3)
            turn(NSEQ - 2)
            load_places(0)
            pe.wait_ge(loaded_experts, 16)
            pe.wait_ge(high_ready, 2 * E)
            pe.wait_ge(low_ready, 2 * E)
            first_at = pe.snap(places[1], min_val=0, max_val=(E - 1) * 2 * HID, out_of_modulus=2 * HID)
            pe.wait_ge(col_ready, 1)
            gate_up(0, first_at, 0, -1)
            gate_up(0, first_at, 1, -1)
            pe.wait_ge(scaled, end)
            pe.wait_ge(q_ready, end - 2)
            turn(NSEQ - 1)
            for n in range(EARLY_PARTS):
                norm_and_route(1, n)
            pe.wait_ge(q_ready, end)
            for run in range(PART_RUNS):
                run_slots(run)
            pe.wait_ge(routed, GROUPS)
            with pe.Fori(PART_RUNS, TILES // RUN - 1) as run:
                run_slots(run)
            last_at = run_slots(TILES // RUN - 1)
            pe.wait_ge(hidden_ready, TILES)
            pe.wait_ge(y_ready, TILES - 1)
            down(TILES - 1, 1, last_at)

        @block.scalar
        def _(act):
            act.wait_ge(const_step, 1)
            nc.scalar.activation(table_scratch[:, :], eps_ln[:, :], ACT.Silu)

            def first_q(b, source):
                act.wait_ge(q0_done, b + 1)
                if b % SG >= 2:
                    act.wait_ge(q0_low_ready, b - 1)
                nc.scalar.activation(first_whole(b), source[:, :], ACT.Identity, bias=b_q[:, 0:1])
                nc.scalar.activation(q_high[:, b, PAD:PAD + LEN], source[:, :], ACT.Identity,
                                     bias=b_q[:, 0:1]).then_inc(q0_ready, 1)

            act.wait_ge(loaded_q, 16)
            for b in range(SG):
                first_q(b, F[b % 2])

            def round_turns(k):
                nc.scalar.activation(turns[:, k, :], F[k][:, :], ACT.Copy, bias=MAGIC).then_inc(rounded, 1)

            def wave(k):
                nc.scalar.activation(waves[:, k, :], turns[:, k, :], ACT.Sin, scale=-TWO_PI).then_inc(waves_ready, 1)

            def take_q(m, b):
                if not isinstance(m, int) or m >= 1:
                    act.wait_ge(q_low_ready, m - b // SG * SG)
                nc.scalar.activation(q_whole, T[b % 2][:, :], ACT.Copy)
                nc.scalar.activation(q_high[:, b, PAD:PAD + LEN], T[b % 2][:, :], ACT.Copy).then_inc(q_ready, 1)

            def take_last_q(b):
                if b == 0:
                    act.wait_ge(filled, 16 * 3)
                if b == SG:
                    act.wait_ge(v_done, SG)
                nc.scalar.activation(q_last[b // SG][:, b % SG * LEN:(b % SG + 1) * LEN], T[b % 2][:, :], ACT.Copy).then_inc(q_ready, 1)

            def split_weights(n):
                e, whole = n // 2, n % 2
                if not 0 <= e < E:
                    return
                if whole:
                    act.wait_ge(high_ready, 2 * e + 1)
                elif e == 0:
                    act.wait_ge(scale_ready, 1)
                nc.scalar.activation((w_raw if whole else w_high)[:, e, :], w_raw[:, e, :], ACT.Copy,
                                     scale=w_scale[:, 0:1]).then_inc(high_ready, 1)

            def norm_and_route(g, n):
                t0, t1 = g * NTG, (g + 1) * NTG
                if n == 8:
                    act.wait_ge(norm_step, t1 + g)
                    nc.scalar.activation(std[:, t0:t1], mean_var[:, t0:t1, 1], ACT.Sqrt, bias=eps_ln[:, 0:1])\
                        .then_inc(std_ready, 1)
                if 2 * SG + 1 <= n < 3 * SG + 1:
                    b = g * SG + n - 2 * SG - 1
                    act.wait_ge(x1T_done, b + 1)
                    if b >= 2:
                        act.wait_ge(gate_read, b - 1)
                    nc.scalar.activation(x1T[:, b % 2, :], bank[6][:, :], ACT.Copy).then_inc(x1T_ready, 1)
                if 11 <= n < 11 + SG:
                    b = n - 11
                    if b == 0 and g == 0:
                        act.wait_ge(filled, 16 * 3)
                    elif b == 0:
                        act.wait_ge(sent, 16 * TOPK * NTG)
                    act.wait_ge(x1_ready, t0 + (b + 1) * CH)
                    nc.scalar.activation(send[:, b * CH:(b + 1) * CH, 0, 0:C // 2].bitcast(F16),
                                         x1[:, t0 + b * CH:t0 + (b + 1) * CH, :], ACT.Copy,
                                         scale=X_SCALE).then_inc(high_sent, 1)
                if n == 16:
                    act.wait_ge(low_sent, (g + 1) * SG)
                    act.dma_start(send[:, :, 1, 0:C], send[:, :, 0, 0:C]).then_inc(rows_step, 16)
                if n == 15:
                    act.wait_ge(shifted_ready, g + 1)
                    nc.scalar.activation(probs[:, :, :], shifted[:, :, :], ACT.Exp).then_inc(exp_done, 1)

            def scan(g):
                first = g * ITEMS
                b0 = g * SG
                for b in range(SG):
                    m = first + b
                    act.wait_ge(f_done, m + 1)
                    if m >= 2:
                        act.wait_ge(waves_ready, m - 1)
                    round_turns(b % 2)
                    if g:
                        split_weights(m - SPLIT_FROM)
                        if b >= PART_FROM:
                            norm_and_route(g - 1, b - PART_FROM)
                    act.wait_ge(turns_ready, m + 1)
                    if m < 2:
                        act.wait_ge(q0_low_ready, m + 3)
                    else:
                        act.wait_ge(z_done, m - 1)
                    wave(b % 2)
                    if m >= 2:
                        act.wait_ge(turned, m - 1)
                        if g and b < 2:
                            take_last_q(b0 + b - 2)
                        else:
                            take_q(m - 2, b0 + b - 2)
                    if m == ITEMS:
                        first_q(NSEQ - 1, bank[7])

                def item(s, b, beside=False, last=False):
                    m = s * SG + (first + b)
                    act.wait_ge(f_done, m + 1)
                    act.wait_ge(waves_ready, m - 1)
                    round_turns(b % 2)
                    if beside:
                        split_weights(m - SPLIT_FROM)
                        if g and m < first + PART_STEPS * SG:
                            norm_and_route(g - 1, m - first - PART_FROM)
                    act.wait_ge(turns_ready, m + 1)
                    act.wait_ge(z_done, m - 1)
                    wave(b % 2)
                    act.wait_ge(turned, m - 1)
                    if last:
                        take_last_q(b0 + b - 2)
                    else:
                        take_q(m - 2, b0 + (b - 2) % SG)

                from_step = 1
                if g:
                    for s in range(1, PART_STEPS):
                        for b in range(SG):
                            item(s, b, beside=True)
                    from_step = PART_STEPS
                split_step = STEPS - 1 if g else SPLIT_FROM // SG
                with act.Fori(from_step, split_step) as s:
                    for b in range(SG):
                        item(s, b)
                for s in range(split_step, STEPS):
                    for b in range(SG):
                        item(s, b, beside=True, last=(s == STEPS - 1 and b >= 2))
                        if g == 0 and s == STEPS - 1 and b >= 1:
                            first_q(SG + b - 1, bank[7 - b % 2])

            for g in range(GROUPS):
                scan(g)

            def silu(k):
                nc.scalar.activation(act_gate[:, k, :], bank[k][:, :], ACT.Silu, scale=unscale[:, 0:1])\
                    .then_inc(act_ready, 1)

            def take_y(i, r, again):
                act.wait_ge(y_done, i + 1)
                act.wait_ge(meta_ready, i + 1)
                if not isinstance(again, int) or again >= 1:
                    act.wait_ge(y_stored[r], again * 16)
                nc.scalar.activation(y_tile[r], bank[5][:, 0:C], ACT.Copy,
                                     scale=meta[:, r, 0:1]).then_inc(y_ready, 1)

            def slot(quad, r):
                i = quad * 4 + r
                if not isinstance(i, int) or i >= 1:
                    act.wait_ge(gate_done, i + 1)
                    if not isinstance(i, int) or i >= 2:
                        act.wait_ge(y_done, i - 1)
                    silu(r % 2)
                if not isinstance(i, int) or i >= 1:
                    take_y(i - 1, (r - 1) % 4, quad if r else quad - 1)
                if isinstance(i, int) and i < PARTS - EARLY_PARTS:
                    norm_and_route(1, i + EARLY_PARTS)

            act.wait_ge(turned, GROUPS * ITEMS - 1)
            take_last_q(NSEQ - 2)
            act.wait_ge(waves_ready, GROUPS * ITEMS)
            nc.scalar.activation(table_scratch[:, :], eps_ln[:, :], ACT.Silu)
            act.wait_ge(gate_done, 1)
            silu(0)
            act.wait_ge(turned, GROUPS * ITEMS)
            take_last_q(NSEQ - 1)
            for quad in range(PART_QUADS):
                for r in range(4):
                    slot(quad, r)
            with act.Fori(PART_QUADS, QUADS) as quad:
                for r in range(4):
                    slot(quad, r)
            take_y(TILES - 1, 3, QUADS - 1)

            act.wait_ge(var_ready, NTG)
            nc.scalar.activation(std2[:, 0:NTG], mean_var2[:, 0:NTG, 1], ACT.Sqrt, bias=eps_ln[:, 0:1])\
                .then_inc(std2_ready, 1)

            def deviation(n):
                t0 = NTG + n * CH
                act.wait_ge(var_ready, t0 + CH)
                nc.scalar.activation(std2[:, t0:t0 + CH], mean_var2[:, t0:t0 + CH, 1], ACT.Sqrt, bias=eps_ln[:, 0:1])\
                    .then_inc(std2_ready, 1)

            def normalise(n):
                act.wait_ge(shift_ready, n + 1)
                for j in range(NTG + n * CH, NTG + (n + 1) * CH):
                    nc.scalar.activation(x1[:, j, :], x1[:, j, :], ACT.Identity, scale=rstd2[:, j:j + 1],
                                         bias=shift2[:, j:j + 1]).then_inc(out_ready_last, 1)

            deviation(0)
            for n in range(SG):
                if n + 1 < SG:
                    deviation(n + 1)
                normalise(n)

        @block.vector
        def _(dve):
            made = [0]

            def const(ins):
                made[0] += 1
                ins.then_inc(const_step, 1)

            def settle():
                dve.wait_ge(const_step, made[0])

            V = nc.vector
            const(V.memset(eps_ln[:, :], EPS_LN))
            const(V.memset(ones_bf[:, :], 1.0))
            const(V.memset(bias_split[:, :, :], 0.0))
            const(V.memset(tile_at[:, 0:1], 0))
            const(V.memset(ones_f[:, :], 1.0))
            dve.wait_ge(iota_done, 1)
            const(V.tensor_scalar(identity[:, :], iota_p[:, :], 0.0, None, ALU.is_equal))
            const(V.tensor_scalar(identity_h[:, :], iota_p[:, :], 0.0, None, ALU.is_equal))
            const(V.tensor_scalar(before[:, :], iota_p[:, :], 0.0, None, ALU.is_gt))
            dve.wait_ge(loaded_q, 16)
            for b in range(NSEQ):
                const(V.tensor_copy(q_high[:, b, 0:PAD], idc[:, 0:1].broadcast_to([P, PAD])))
            dve.wait_ge(loaded_freq, 16 * 2)
            const(V.tensor_scalar(bias_row[:, 0, 0:P // 2], bias_row[:, 0, 0:P // 2], INV_TWO_PI, None, ALU.mult))
            const(V.tensor_scalar(bias_row[:, 0, P // 2:P], bias_row[:, 0, P // 2:P], INV_TWO_PI, 0.25, ALU.mult,
                                  ALU.add))
            const(V.tensor_scalar(w_freq_raw, w_freq_raw, INV_TWO_PI, None, ALU.mult))
            settle()
            const(V.tensor_copy(bias_split[0:1, :, :], bias_row[:, :, :]))
            const(V.tensor_copy(w_freq_high[:, :, :], w_freq_raw))
            settle()
            const(V.tensor_tensor(bias_left[:, 0, :, :], bias_row[:, :, :], bias_split[0:1, :, :], ALU.subtract))
            const(V.tensor_tensor(w_freq_low[:, :, :], w_freq_raw, w_freq_high[:, :, :].bitcast(F32), ALU.subtract))
            settle()
            const(V.tensor_copy(bias_split[32:33, :, :], bias_left[:, 0, :, :]))
            settle()
            const(V.tensor_copy(bias_left[:, 1, :, :], bias_split[32:33, :, :]))
            settle()
            const(V.tensor_tensor(bias_left[:, 1, :, :], bias_left[:, 0, :, :], bias_left[:, 1, :, :], ALU.subtract))
            settle()
            const(V.tensor_copy(bias_split[64:65, :, :], bias_left[:, 1, :, :]))
            settle()
            for b in range(SG):
                V.tensor_tensor(q_low[:, b, 0:PAD], idc[:, 0:1].broadcast_to([P, PAD]),
                                q_high[:, b, 0:PAD].bitcast(F32), ALU.subtract).then_inc(consts_ready, 1)

            def take_turns(k):
                V.scalar_tensor_tensor(out=turns[:, k, :], in0=turns[:, k, :], scalar=-MAGIC,
                                       in1=F[k][:, :], op0=ALU.add, op1=ALU.subtract).then_inc(turns_ready, 1)

            def scale(m, k):
                z = Z[k][:, :].rearrange("p (t c) -> p t c", c=C)
                V.tensor_reduce(z_max[:, k, :], z, AX.X, ALU.max, apply_absolute_value=True).then_inc(scale_step, 1)
                dve.wait_ge(scale_step, m * 3 + 1)
                V.tensor_scalar(z_max_eps[:, k, :], z_max[:, k, :], EPS_MAX, None, ALU.add).then_inc(scale_step, 1)
                dve.wait_ge(scale_step, m * 3 + 2)
                V.reciprocal(z_inv[:, k, :], z_max_eps[:, k, :]).then_inc(scale_step, 1)
                dve.wait_ge(scale_step, m * 3 + 3)
                V.tensor_tensor(z_scaled[:, k, :, :], z, z_inv[:, k, :].unsqueeze(2).broadcast_to([P, CH, C]),
                                ALU.mult).then_inc(scaled, 1)

            def take_low(m, b):
                dve.wait_ge(q_ready, m + 1)
                V.tensor_tensor(q_low[:, b % SG, PAD:PAD + LEN], q_whole, q_high[:, b, PAD:PAD + LEN].bitcast(F32),
                                ALU.subtract).then_inc(q_low_ready, 1)

            def weight_scale():
                dve.wait_ge(w_step, E)
                V.tensor_reduce(w_max[:, :], w_max_e[:, :], AX.X, ALU.max).then_inc(max_ready, 1)

            def weight_scale_end():
                dve.wait_ge(max_all, 1)
                V.tensor_scalar(w_power[:, :].bitcast(I32), w_max_all[:, :].bitcast(I32), 0x7F800000, None,
                                ALU.bitwise_and).then_inc(w_step, 1)
                dve.wait_ge(w_step, E + 1)
                V.tensor_scalar(w_power[:, :], w_power[:, :], 2.0 ** -100, None, ALU.max).then_inc(w_step, 1)
                dve.wait_ge(w_step, E + 2)
                V.reciprocal(w_inv[:, :], w_power[:, :]).then_inc(w_step, 1)
                V.tensor_scalar(unscale[:, :], w_power[:, :], 1.0 / (W_TOP * X_SCALE), None, ALU.mult)\
                    .then_inc(w_step, 1)
                dve.wait_ge(w_step, E + 4)
                V.tensor_scalar(w_scale[:, :], w_inv[:, :], W_TOP, None, ALU.mult).then_inc(scale_ready, 1)

            step = [0]

            def start(ins):
                step[0] += 1
                ins.then_inc(route_step, 1)

            def link(ins):
                start(ins)
                dve.wait_ge(route_step, step[0])

            def over_e(x):
                return x.unsqueeze(2).broadcast_to([P, NTG, E])

            def gate_q(b):
                dve.wait_ge(q_ready, (b // SG + 1) * ITEMS - SG + b % SG + 1)
                dve.wait_ge(v_done, b + 1)
                if b == 0:
                    dve.wait_ge(q0_low_ready, NSEQ)
                if b >= 2:
                    dve.wait_ge(proj_done, b - 1)
                V.scalar_tensor_tensor(out=gated[:, b % 2, :], in0=bank[6][:, :], scalar=b_v[:, 0:1],
                                       in1=q_last[b // SG][:, b % SG * LEN:(b % SG + 1) * LEN],
                                       op0=ALU.add, op1=ALU.mult).then_inc(gated_ready, 1)

            def add_x(b):
                if b == 0:
                    dve.wait_ge(loaded_rows, 16)
                dve.wait_ge(proj_done, b + 1)
                rows = x1[:, b * CH:(b + 1) * CH, :].rearrange("p t c -> p (t c)")
                V.tensor_tensor(rows, bank[7][:, :], rows, ALU.add).then_inc(res_ready, 1)
                dve.wait_ge(res_ready, b + 1)
                for j in range(b * CH, (b + 1) * CH):
                    V.bn_stats(stats[:, j, :], x1[:, j, :]).then_inc(stats_step, 1)
                for j in range(b * CH, (b + 1) * CH):
                    dve.wait_ge(stats_step, j + 1)
                    V.bn_aggr(mean_var[:, j, :], stats[:, j, :]).then_inc(norm_step, 1)

            def choose(k, values, col_read=None):
                link(V.tensor_tensor(work[:, :, :], values, over_e(col[:, :]), ALU.is_equal))
                link(V.tensor_tensor(work[:, :, :], work[:, :, :], rank_key[:, :, :], ALU.mult))
                if col_read:
                    dve.wait_ge(*col_read)
                link(V.tensor_reduce(col[:, :], work[:, :, :], AX.X, ALU.max))
                link(V.tensor_tensor(pick[k][:, :, :], rank_key[:, :, :], over_e(col[:, :]), ALU.is_equal))

            def norm_and_route(g, n):
                t0, t1 = g * NTG, (g + 1) * NTG
                if n < 2 * SG:
                    (gate_q, add_x)[n % 2](g * SG + n // 2)
                if n == 2 * SG:
                    dve.wait_ge(std_ready, g + 1)
                    V.reciprocal(rstd[:, t0:t1], std[:, t0:t1]).then_inc(norm_step, 1)
                    dve.wait_ge(norm_step, t1 + g + 1)
                if 2 * SG <= n < 3 * SG:
                    b = g * SG + n - 2 * SG
                    for j in range(b * CH, (b + 1) * CH):
                        V.tensor_scalar(x1[:, j, :], x1[:, j, :], mean_var[:, j, 0:1], rstd[:, j:j + 1],
                                        ALU.subtract, ALU.mult).then_inc(x1_ready, 1)
                if 12 <= n < 12 + SG:
                    b = n - 12
                    dve.wait_ge(high_sent, g * SG + b + 1)
                    dve.wait_ge(x1_ready, t0 + (b + 1) * CH)
                    V.scalar_tensor_tensor(out=send[:, b * CH:(b + 1) * CH, 0, C // 2:C].bitcast(F16),
                                           in0=x1[:, t0 + b * CH:t0 + (b + 1) * CH, :], scalar=X_SCALE,
                                           in1=send[:, b * CH:(b + 1) * CH, 0, 0:C // 2].bitcast(F16), op0=ALU.mult,
                                           op1=ALU.subtract).then_inc(low_sent, 1)
                if n == 14:
                    dve.wait_ge(gate_read, (g + 1) * SG)
                    dve.wait_ge(iota_done, 3)
                    link(V.tensor_reduce(col[:, :], logits, AX.X, ALU.max))
                    V.tensor_tensor(shifted[:, :, :], logits, over_e(col[:, :]), ALU.subtract)\
                        .then_inc(shifted_ready, 1)
                    choose(0, logits, col_read=(shifted_ready, g + 1))
                if n == 15:
                    link(V.scalar_tensor_tensor(out=masked[:, :, :], in0=pick[0][:, :, :], scalar=NEG,
                                                in1=logits, op0=ALU.mult, op1=ALU.add))
                    link(V.tensor_reduce(col[:, :], masked[:, :, :], AX.X, ALU.max))
                    choose(1, masked[:, :, :])
                    V.tensor_tensor(picked[:, :, :], pick[0][:, :, :], pick[1][:, :, :], ALU.add)\
                        .then_inc(picked_ready, 1)
                if n == 16:
                    dve.wait_ge(exp_done, g + 1)
                    link(V.tensor_reduce(col[:, :], probs[:, :, :], AX.X, ALU.add))
                    link(V.reciprocal(wsum[:, :], col[:, :]))
                    link(V.tensor_tensor(probs[:, :, :], probs[:, :, :], over_e(wsum[:, :]), ALU.mult))
                    start(V.tensor_tensor(work[:, :, :], probs[:, :, :], pick[0][:, :, :], ALU.mult))
                    link(V.tensor_tensor(masked[:, :, :], probs[:, :, :], pick[1][:, :, :], ALU.mult))
                    start(V.tensor_reduce(weight_raw[:, 0, :], work[:, :, :], AX.X, ALU.add))
                    link(V.tensor_reduce(weight_raw[:, 1, :], masked[:, :, :], AX.X, ALU.add))
                if n == 17:
                    link(V.tensor_tensor(col[:, :], weight_raw[:, 0, :], weight_raw[:, 1, :], ALU.add))
                    link(V.reciprocal(wsum[:, :], col[:, :]))
                    dve.wait_ge(high_sent, (g + 1) * SG)
                    for k in range(TOPK):
                        start(V.tensor_tensor(send[:, :, k, C], weight_raw[:, k, :], wsum[:, :], ALU.mult))
                    dve.wait_ge(target_ready, 1)
                    V.tensor_copy(send[:, :, :, C + 1].bitcast(U32), target[:, t0:t1, :]).then_inc(moved, 1)
                if n == 18:
                    dve.wait_ge(counts_done, 2 * (g + 1))
                    for e in range(E):
                        V.tensor_tensor_scan(out=count_to[:, :, e], data0=ones_f[:, 0:NTG], data1=tile_count[:, :, e],
                                             initial=0.0, op0=ALU.mult, op1=ALU.add).then_inc(scan_step, 1)
                    dve.wait_ge(scan_step, E * (g + 1))
                    link(V.tensor_scalar(e_tiles[:, :], count_to[:, NTG - 1, :], 1.0 / P, (P / 2 - 0.5) / P, ALU.mult,
                                         ALU.add))
                    link(V.tensor_scalar(e_tiles_r[:, :], e_tiles[:, :], MAGIC, None, ALU.add))
                    link(V.tensor_scalar(e_tiles[:, :], e_tiles_r[:, :], -MAGIC, None, ALU.add))
                    link(V.tensor_tensor_scan(out=e_end[:, :], data0=ones_f[:, 0:E], data1=e_tiles[:, :], initial=0.0,
                                              op0=ALU.mult, op1=ALU.add))
                if n == 19:
                    start(V.tensor_tensor(e_base[:, :], e_end[:, :], e_tiles[:, :], ALU.subtract))
                    link(V.tensor_tensor(place[:, :, :], count_to[:, :, :], tile_count, ALU.subtract))
                    start(V.tensor_tensor(place[:, :, :], before_in_tile, place[:, :, :], ALU.add))
                    link(V.tensor_scalar(e_base[:, :], e_base[:, :], float(P), float(g * TG * P), ALU.mult, ALU.add))
                    link(V.tensor_tensor(place[:, :, :], place[:, :, :],
                                         e_base[:, :].unsqueeze(1).broadcast_to([P, NTG, E]), ALU.add))
                    start(V.tensor_tensor(work[:, :, :], place[:, :, :], pick[0][:, :, :], ALU.mult))
                    link(V.tensor_tensor(masked[:, :, :], place[:, :, :], pick[1][:, :, :], ALU.mult))
                    start(V.tensor_reduce(pos_f[:, 0, t0:t1], work[:, :, :], AX.X, ALU.add))
                    link(V.tensor_reduce(pos_f[:, 1, t0:t1], masked[:, :, :], AX.X, ALU.add))
                    dve.wait_ge(rows_step, 16 * (g + 1))
                    dve.wait_ge(moved, g + 1)
                    V.tensor_copy(pos[:, :, t0:t1], pos_f[:, :, t0:t1]).then_inc(rows_ready, 1)
                if n == PARTS - 1:
                    link(V.tensor_tensor(tile_ge[:, :, :], tile_no[:, :, :],
                                         e_end[0:1, :].unsqueeze(1).broadcast_to([1, TG, E]), ALU.is_ge))
                    link(V.tensor_reduce(tile_expert_f[:, :], tile_ge[:, :, :], AX.X, ALU.add))
                    V.tensor_scalar(tile_at[:, 1 + g * TG:1 + (g + 1) * TG], tile_expert_f[:, :], float(E - 1),
                                    float(2 * HID), ALU.min, ALU.mult).then_inc(routed, 1)
                    dve.wait_ge(routed, g + 1)

            def scan(g):
                first = g * ITEMS
                for b in range(SG):
                    m = first + b
                    dve.wait_ge(rounded, m + 1)
                    if m >= 2:
                        dve.wait_ge(waves_ready, m - 1)
                    take_turns(b % 2)
                    if m >= 1:
                        dve.wait_ge(z_done, m)
                        if m >= 3:
                            dve.wait_ge(turned, m - 2)
                        scale(m - 1, (b - 1) % 2)
                    if m < SG:
                        V.memset(send[:, b * CH:(b + 1) * CH, :, :], 0.0).then_inc(blank_ready, 1)
                    if g and b >= PART_FROM:
                        norm_and_route(g - 1, b - PART_FROM)

                def item(s, b):
                    m = s * SG + (first + b)
                    dve.wait_ge(rounded, m + 1)
                    dve.wait_ge(waves_ready, m - 1)
                    take_turns(b % 2)
                    dve.wait_ge(z_done, m)
                    dve.wait_ge(turned, m - 2)
                    scale(m - 1, (b - 1) % 2)

                def looped(s0, s1):
                    with dve.Fori(s0, s1) as s:
                        for b in range(SG):
                            item(s, b)

                if g == 0:
                    looped(1, MAX_FROM)
                    dve.wait_ge(loaded_gate_up, 16)
                    with dve.Fori(MAX_FROM, MAX_FROM + MAX_STEPS) as s:
                        for b in range(SG):
                            item(s, b)
                            if b % 2:
                                e = s * 2 + (b // 2 - 2 * MAX_FROM)
                                V.tensor_reduce(w_max_e[:, bass.ds(e, 1)],
                                                w_raw[:, bass.ds(e, 1), :].rearrange("p a n -> p (a n)"), AX.X,
                                                ALU.max, apply_absolute_value=True).then_inc(w_step, 1)
                    for b in range(SG):
                        if b == 0:
                            weight_scale()
                        item(MAX_FROM + MAX_STEPS, b)
                        if b == 2:
                            weight_scale_end()
                    looped(MAX_FROM + MAX_STEPS + 1, STEPS)
                else:
                    for s in range(1, PART_STEPS):
                        for b in range(SG):
                            item(s, b)
                            norm_and_route(g - 1, s * SG + b - PART_FROM)
                    for s in range(PART_STEPS, STEPS):
                        for b in range(SG):
                            done = s * SG + b - 3
                            if LOW_BY_DVE <= done < ITEMS - SG:
                                take_low(first + done, SG + done % SG)
                            item(s, b)

            for g in range(GROUPS):
                scan(g)

            def take_cols(i, k, r, again):
                dve.wait_ge(row_turned, i + 1)
                if not isinstance(i, int) or i >= 2:
                    dve.wait_ge(up_done, i - 1)
                V.tensor_copy(col_tile[:, k, :, :].rearrange("p a n -> p (a n)"),
                              bank[6 if isinstance(i, int) and i == 0 else 4][:, 0:P].bitcast(F16))\
                    .then_inc(col_ready, 1)
                if not isinstance(again, int) or again >= 1:
                    dve.wait_ge(y_stored[r], again * 16)
                V.tensor_copy(meta[:, r, :].bitcast(U32), row_tile[:, k, C:ROW].bitcast(U32)).then_inc(meta_ready, 1)

            def slot(quad, r, last=False):
                i = quad * 4 + r
                k = r % 2
                if not last:
                    take_cols(i + 1, 1 - k, (r + 1) % 4, quad if r < 3 else quad + 1)
                dve.wait_ge(act_ready, i + 1)
                dve.wait_ge(up_done, i + 1)
                V.scalar_tensor_tensor(out=hidden[:, k, :], in0=bank[2 + k][:, :], scalar=unscale[:, 0:1],
                                       in1=act_gate[:, k, :], op0=ALU.mult, op1=ALU.mult).then_inc(hidden_ready, 1)
                if isinstance(i, int) and i < PARTS - EARLY_PARTS:
                    norm_and_route(1, i + EARLY_PARTS)

            def add_up(pair, k, fetched):
                dve.wait_ge(y_fetched[k], fetched * 16)
                V.tensor_tensor(y_sum[:, k, :, :], y_back[:, k, :, 0, :], y_back[:, k, :, 1, :], ALU.add)\
                    .then_inc(y_summed, 1)
                dve.wait_ge(y_summed, pair + 1)
                V.tensor_tensor(x1[:, bass.ds(pair * 2, 2), :], x1[:, bass.ds(pair * 2, 2), :], y_sum[:, k, :, :],
                                ALU.add).then_inc(merged, 1)
                dve.wait_ge(merged, pair + 1)
                for n in range(2):
                    V.bn_stats(stats2[:, bass.ds(pair * 2 + n, 1), :].rearrange("p a n -> p (a n)"),
                               x1[:, bass.ds(pair * 2 + n, 1), :].rearrange("p a n -> p (a n)"))\
                        .then_inc(stats2_ready, 1)

            take_cols(0, 0, 0, 0)
            end = GROUPS * ITEMS
            dve.wait_ge(z_done, end)
            dve.wait_ge(turned, end - 2)
            scale(end - 1, (SG - 1) % 2)
            for n in range(EARLY_PARTS):
                norm_and_route(1, n)
            for quad in range(PART_QUADS):
                for r in range(4):
                    slot(quad, r)
            with dve.Fori(PART_QUADS, TG // 4 + 2) as quad:
                for r in range(4):
                    slot(quad, r)
            with dve.Fori(0, NTG // 4 - 1) as n:
                for k in range(2):
                    quad = n * 2 + (k + TG // 4 + 2)
                    for r in range(4):
                        slot(quad, r)
                    add_up(n * 2 + k, k, n + 1)
            quad = QUADS - 2
            for r in range(4):
                slot(quad, r)
            add_up(NTG // 2 - 2, 0, NTG // 4)
            for r in range(4):
                slot(QUADS - 1, r, last=(r == 3))
            add_up(NTG // 2 - 1, 1, NTG // 4)
            for j in range(NTG):
                dve.wait_ge(stats2_ready, j + 1)
                V.bn_aggr(mean_var2[:, j, :], stats2[:, j, :]).then_inc(var_ready, 1)
            dve.wait_ge(std2_ready, 1)
            V.reciprocal(rstd2[:, 0:NTG], std2[:, 0:NTG]).then_inc(rstd2_ready, 1)
            dve.wait_ge(rstd2_ready, 1)
            for j in range(NTG):
                V.tensor_scalar(x1[:, j, :], x1[:, j, :], mean_var2[:, j, 0:1], rstd2[:, j:j + 1],
                                ALU.subtract, ALU.mult).then_inc(out_ready, 1)

            def norm_scale(n):
                t0 = NTG + n * CH
                dve.wait_ge(std2_ready, n + 2)
                V.reciprocal(rstd2[:, t0:t0 + CH], std2[:, t0:t0 + CH]).then_inc(rstd2_ready, 1)
                dve.wait_ge(rstd2_ready, n + 2)
                V.scalar_tensor_tensor(out=shift2[:, t0:t0 + CH], in0=mean_var2[:, t0:t0 + CH, 0], scalar=-1.0,
                                       in1=rstd2[:, t0:t0 + CH], op0=ALU.mult, op1=ALU.mult).then_inc(shift_ready, 1)

            for n in range(SG):
                t0 = NTG + n * CH
                dve.wait_ge(y_last_summed, n + 1)
                V.tensor_tensor(x1[:, t0:t0 + CH, :], x1[:, t0:t0 + CH, :], y_last[:, n, :, 0, :], ALU.add)\
                    .then_inc(merged, 1)
                dve.wait_ge(merged, NTG // 2 + n + 1)
                for j in range(t0, t0 + CH):
                    V.bn_stats(stats2[:, j, :], x1[:, j, :]).then_inc(stats2_ready, 1)
                if n:
                    norm_scale(n - 1)
                for j in range(t0, t0 + CH):
                    dve.wait_ge(stats2_ready, j + 1)
                    V.bn_aggr(mean_var2[:, j, :], stats2[:, j, :]).then_inc(var_ready, 1)
            norm_scale(SG - 1)


def kernel(**inputs):
    import numpy as np
    import concourse.bacc as bacc
    from concourse.bass_utils import run_bass_kernel_spmd

    a = {k: np.asarray(v) for k, v in inputs.items()}
    x = a["L0_attn_x"].reshape(NT * P, C)
    fw = a["L0_attn_freq_W"].reshape(2, C, P // 2)
    fb = a["L0_attn_freq_b"]
    host = {
        "x_rows": x.reshape(NT, P, C).transpose(1, 0, 2),
        "x_cols": x.T,
        "attn_params": np.concatenate([a["L0_attn_attn_W"], a["L0_attn_attn_b"].reshape(2, C).T,
                                       a["L0_attn_identity"].reshape(C, 1)], axis=1),
        "weights": np.concatenate([fw[0], fw[0], fw[1], fw[1], a["L0_attn_out_W"], a["L0_attn_proj_W"],
                                   a["L0_ffn_gate_w"].T], axis=1),
        "biases": np.stack([np.concatenate([fb, fb]), a["L0_attn_out_b"], a["L0_attn_proj_b"]]).reshape(1, 3, P),
        "gu_T": a["L0_ffn_gate_up_proj"].transpose(2, 0, 1),
        "dn_T": a["L0_ffn_down_proj"].transpose(0, 2, 1).reshape(E, HC, P, C).transpose(2, 0, 1, 3),
    }
    nc = bacc.Bacc("TRN2", target_bir_lowering=False, num_devices=1)
    arrays, args = {}, []
    for name, v in host.items():
        v = np.ascontiguousarray(v)
        arrays[name] = v
        args.append(nc.dram_tensor(name, v.shape, mybir.dt.from_np(v.dtype), kind="ExternalInput").ap())
    out = nc.dram_tensor("out_rows", (NT * P, C), F32, kind="ExternalOutput").ap()
    build(nc, *args, out)
    r = run_bass_kernel_spmd(nc, [arrays], core_ids=[0])
    return r.results[0]["out_rows"].reshape(NSEQ, LEN, C)
```
